# Optimizing a Trainium2 kernel written in Bass

```python
import numpy as np
import jax
import jax.numpy as jnp

def _softmax(x, axis=-1):
    return jax.nn.softmax(x, axis=axis)

def _gelu(x):
    return jax.nn.gelu(x, approximate=True)

def _silu(x):
    return jax.nn.silu(x)

def _sigmoid(x):
    return jax.nn.sigmoid(x)

def _layernorm(x, axis=-1, eps=1e-05):
    m = jnp.mean(x, axis=axis, keepdims=True)
    v = jnp.var(x, axis=axis, keepdims=True)
    return (x - m) / jnp.sqrt(v + eps)

def _scatter_add(tgt, idx, src, axis=0):
    return tgt.at[idx].add(src)

def _segment_sum(src, seg, n):
    return jax.ops.segment_sum(src, seg, n)
kernel_name = 'mk_gnn_ffn_d1_gnn_r16_4557c0'

def setup_inputs(seed: int=0):
    np.random.seed(seed)
    _w = jnp.asarray

    def _rec_inputs():
        import jax
        import jax.numpy as jnp
        _gk = jax.random.key(seed)
        x = -0.0003713 + 1 * jax.random.normal(jax.random.fold_in(_gk, 1), (3125, 256), jnp.float32)
        src = jax.random.randint(jax.random.fold_in(_gk, 2), (50000,), 0, 3125, jnp.int32)
        dst = jax.random.randint(jax.random.fold_in(_gk, 3), (50000,), 0, 3125, jnp.int32)
        _o = jnp.argsort(dst, stable=True)
        src = src[_o]
        dst = dst[_o]
        edge_type_64 = jax.random.randint(jax.random.fold_in(_gk, 12), (50000,), 0, 64, jnp.int32)
        return (x, src, dst, edge_type_64)
    x, src, dst, edge_type_64 = _rec_inputs()

    def _L0_gnn_setup():
        import jax, jax.numpy as jnp
        import numpy as np
        N_NODES = 3125
        N_EDGES = 31250
        IN_DIM = 256
        HID = 64
        HEADS = 4
        N_REL = 64
        key = jax.random.key(seed)
        ks = jax.random.split(key, 16)
        s = 0.02
        return {'node_features': jax.random.normal(ks[0], (N_NODES, IN_DIM), jnp.float32), 'edge_index': jax.random.randint(ks[1], (2, N_EDGES), 0, N_NODES, jnp.int32), 'edge_relations': jax.random.randint(ks[2], (N_EDGES,), 0, N_REL, jnp.int32), 'query_emb': jax.random.normal(ks[3], (IN_DIM,), jnp.float32), 'Wq': jax.random.normal(ks[4], (IN_DIM, HID * HEADS), jnp.float32) * s, 'bq': jnp.zeros((HID * HEADS,), jnp.float32), 'Wk': jax.random.normal(ks[5], (IN_DIM, HID * HEADS), jnp.float32) * s, 'bk': jnp.zeros((HID * HEADS,), jnp.float32), 'Wv': jax.random.normal(ks[6], (IN_DIM, HID * HEADS), jnp.float32) * s, 'bv': jnp.zeros((HID * HEADS,), jnp.float32), 'rel_w': jax.random.normal(ks[7], (N_REL, HID), jnp.float32) * s, 'Wo': jax.random.normal(ks[8], (HID * HEADS, IN_DIM), jnp.float32) * s, 'bo': jnp.zeros((IN_DIM,), jnp.float32), 'gamma': jnp.ones((IN_DIM,), jnp.float32), 'beta': jnp.zeros((IN_DIM,), jnp.float32)}
    _L0_gnn_all = _L0_gnn_setup()
    _L0_gnn_in = {k: v for k, v in _L0_gnn_all.items() if k in ('query_emb', 'Wq', 'bq', 'Wk', 'bk', 'Wv', 'bv', 'rel_w', 'Wo', 'bo', 'gamma', 'beta')}
    del _L0_gnn_all

    def _L0_ffn_setup():
        import jax, jax.numpy as jnp
        import numpy as np
        D_MODEL = 256
        N_EXPERTS = 16
        HIDDEN = 512
        SCALE = 0.02
        key = jax.random.key(seed)
        ks = jax.random.split(key, 5)
        x = jax.random.normal(ks[0], (4, 512, D_MODEL), dtype=jnp.float32)
        gate_w = jax.random.normal(ks[1], (D_MODEL, N_EXPERTS), dtype=jnp.float32) * SCALE
        gate_b = jnp.zeros((N_EXPERTS,), dtype=jnp.float32)
        w1 = jax.random.normal(ks[2], (N_EXPERTS, D_MODEL, HIDDEN), dtype=jnp.float32) * SCALE
        w2 = jax.random.normal(ks[3], (N_EXPERTS, D_MODEL, HIDDEN), dtype=jnp.float32) * SCALE
        w3 = jax.random.normal(ks[4], (N_EXPERTS, HIDDEN, D_MODEL), dtype=jnp.float32) * SCALE
        return {'x': x, 'gate_w': gate_w, 'gate_b': gate_b, 'w1': w1, 'w2': w2, 'w3': w3}
    _L0_ffn_all = _L0_ffn_setup()
    _L0_ffn_in = {k: v for k, v in _L0_ffn_all.items() if k in ('gate_w', 'gate_b', 'w1', 'w2', 'w3')}
    del _L0_ffn_all
    return {'x': x, 'src': src, 'dst': dst, 'edge_type_64': edge_type_64, 'L0_gnn_query_emb': _L0_gnn_in['query_emb'], 'L0_gnn_Wq': _L0_gnn_in['Wq'], 'L0_gnn_bq': _L0_gnn_in['bq'], 'L0_gnn_Wk': _L0_gnn_in['Wk'], 'L0_gnn_bk': _L0_gnn_in['bk'], 'L0_gnn_Wv': _L0_gnn_in['Wv'], 'L0_gnn_bv': _L0_gnn_in['bv'], 'L0_gnn_rel_w': _L0_gnn_in['rel_w'], 'L0_gnn_Wo': _L0_gnn_in['Wo'], 'L0_gnn_bo': _L0_gnn_in['bo'], 'L0_gnn_gamma': _L0_gnn_in['gamma'], 'L0_gnn_beta': _L0_gnn_in['beta'], 'L0_ffn_gate_w': _L0_ffn_in['gate_w'], 'L0_ffn_gate_b': _L0_ffn_in['gate_b'], 'L0_ffn_w1': _L0_ffn_in['w1'], 'L0_ffn_w2': _L0_ffn_in['w2'], 'L0_ffn_w3': _L0_ffn_in['w3']}

def reference(x, src, dst, edge_type_64, L0_gnn_query_emb, L0_gnn_Wq, L0_gnn_bq, L0_gnn_Wk, L0_gnn_bk, L0_gnn_Wv, L0_gnn_bv, L0_gnn_rel_w, L0_gnn_Wo, L0_gnn_bo, L0_gnn_gamma, L0_gnn_beta, L0_ffn_gate_w, L0_ffn_gate_b, L0_ffn_w1, L0_ffn_w2, L0_ffn_w3):
    import jax
    import jax.numpy as jnp

    def _L0_gnn_ref(node_features, edge_index, edge_relations, query_emb, Wq, bq, Wk, bk, Wv, bv, rel_w, Wo, bo, gamma, beta):
        import jax, jax.numpy as jnp
        import numpy as np
        N_NODES = 3125
        N_EDGES = 31250
        IN_DIM = 256
        HID = 64
        HEADS = 4
        N_REL = 64
        N = node_features.shape[0]
        D = rel_w.shape[1]
        H = Wq.shape[1] // D
        enh = node_features + 0.1 * query_emb[None, :]
        Q = (enh @ Wq + bq).reshape(N, H, D)
        K = (enh @ Wk + bk).reshape(N, H, D)
        V = (enh @ Wv + bv).reshape(N, H, D)
        src, dst = (edge_index[0], edge_index[1])
        rel = rel_w[edge_relations]
        mod_k = K[src] + 0.2 * rel[:, None, :]
        scores = jnp.einsum('ehd,ehd->eh', Q[dst], mod_k) / D ** 0.5
        seg_max = jax.ops.segment_max(scores, dst, num_segments=N)
        ex = jnp.exp(scores - seg_max[dst])
        denom = jax.ops.segment_sum(ex, dst, num_segments=N)
        w = ex / denom[dst]
        agg = jax.ops.segment_sum(w[:, :, None] * V[src], dst, num_segments=N)
        deg = jax.ops.segment_sum(jnp.ones((src.shape[0],), jnp.float32), dst, num_segments=N)
        msgs = jnp.where(deg[:, None, None] > 0, agg, V)
        out = msgs.reshape(N, H * D) @ Wo + bo
        x = out + node_features
        mu = jnp.mean(x, axis=-1, keepdims=True)
        var = jnp.var(x, axis=-1, keepdims=True)
        return (x - mu) / jnp.sqrt(var + 1e-05) * gamma + beta

    def _L0_ffn_ref(x, gate_w, gate_b, w1, w2, w3):
        import jax, jax.numpy as jnp
        import numpy as np
        D_MODEL = 256
        N_EXPERTS = 16
        HIDDEN = 512
        SCALE = 0.02
        n_experts = w1.shape[0]
        logits = jnp.einsum('bsd,de->bse', x, gate_w) + gate_b
        probs = jax.nn.softmax(logits, axis=-1)
        top_probs, top_idx = jax.lax.top_k(probs, 2)
        top_probs = top_probs / jnp.sum(top_probs, axis=-1, keepdims=True)
        dispatch = jnp.sum(jax.nn.one_hot(top_idx, n_experts, dtype=x.dtype) * top_probs[..., None], axis=-2)
        h1 = jnp.einsum('bsd,edh->bseh', x, w1)
        h2 = jnp.einsum('bsd,edh->bseh', x, w2)
        hidden = jax.nn.silu(h1) * h2
        expert_out = jnp.einsum('bseh,eho->bseo', hidden, w3)
        return jnp.einsum('bseo,bse->bso', expert_out, dispatch)
    edge_index = jnp.stack([src, dst])
    x = x + _L0_gnn_ref(_layernorm(x, axis=-1), edge_index, edge_type_64, L0_gnn_query_emb, L0_gnn_Wq, L0_gnn_bq, L0_gnn_Wk, L0_gnn_bk, L0_gnn_Wv, L0_gnn_bv, L0_gnn_rel_w, L0_gnn_Wo, L0_gnn_bo, L0_gnn_gamma, L0_gnn_beta)
    x = x + _L0_ffn_ref(_layernorm(x, axis=-1)[None], L0_ffn_gate_w, L0_ffn_gate_b, L0_ffn_w1, L0_ffn_w2, L0_ffn_w3)[0]
    return x

_drawn_inputs = setup_inputs


def setup_inputs(seed=0):
    import zlib

    import numpy as np

    out = dict(_drawn_inputs(seed))
    spreads = {'L0_gnn_bq': (0.0, 0.8),
     'L0_gnn_bk': (0.0, 0.8),
     'L0_gnn_bv': (0.0, 0.502),
     'L0_gnn_bo': (0.0, 0.1),
     'L0_gnn_gamma': (1.0, 0.2),
     'L0_gnn_beta': (0.0, 0.1),
     'L0_ffn_gate_b': (0.0, 0.8)}
    factors = {'L0_gnn_query_emb': 8.0,
     'L0_gnn_Wq': 8.0,
     'L0_gnn_Wk': 8.0,
     'L0_gnn_Wv': 4.02,
     'L0_gnn_rel_w': 8.0,
     'L0_gnn_Wo': 2.691,
     'L0_ffn_gate_w': 7.29,
     'L0_ffn_w1': 6.705,
     'L0_ffn_w2': 6.628,
     'L0_ffn_w3': 6.615}
    for name, (base, spread) in spreads.items():
        noise = np.random.default_rng([zlib.crc32(name.encode()), seed]).standard_normal(out[name].shape)
        drawn = base * np.exp(spread * noise) if base else spread * noise
        out[name] = jnp.asarray(drawn.astype(out[name].dtype))
    for name, factor in factors.items():
        out[name] = (out[name] * factor).astype(out[name].dtype)
    return out
```

```python
from contextlib import ExitStack

import concourse.bass as bass
from concourse import mybir

F32 = mybir.dt.float32
BF16 = mybir.dt.bfloat16
I32 = mybir.dt.int32
U32 = mybir.dt.uint32
ALU = mybir.AluOpType
ACT = mybir.ActivationFunctionType
AX = mybir.AxisListType

P = 128
N = 3125
D = 256
H = 4
HD = 64
R = 64
E = 50000
NX = 16
HID = 512
KC = D // P
HC = HID // P
NODE_TILES = -(-N // P)
NT = NODE_TILES + 1
NP = NT * P
XT = NT + 1
EP = 98
EQ = 4
ET = EP * EQ
SP_ = 104
STEPS = SP_ * 4
assert -(-E // P) + NODE_TILES - 1 <= STEPS and ET * P >= E
NO_DST = 1 << 20
BIG = 1.0e30
EPS = 1e-5
GRP = 16
STG = 8
AHEAD = 3
PAIRS = GRP // 2
TURNS = STEPS // GRP
BLOCKS = (2 * N + NX * (P - 1)) // P
YROWS = BLOCKS * P


class Stage:

    def __init__(self, sem, credit=8):
        self.sem, self.credit = sem, credit

    def hold(self, eng, n, pin):
        self.wait(eng, n)
        eng.sem_inc(pin, 1)

    def open(self, eng):
        eng.sem_inc(self.sem, self.credit)

    def wait(self, eng, n):
        eng.wait_ge(self.sem, n + (1 + self.credit))


class Event:

    def __init__(self, sem):
        self.sem = sem

    def set(self, eng):
        eng.sem_inc(self.sem, 1)

    def wait(self, eng):
        eng.wait_ge(self.sem, 1)


class Chain:

    def __init__(self, eng, sem):
        self.eng, self.sem, self.n = eng, sem, 0

    def __call__(self, ins):
        self.n += 1
        ins.then_inc(self.sem, 1)
        self.eng.wait_ge(self.sem, self.n)


def build(nc, A, out):
    ctx = ExitStack()
    with ctx:
        def sb(name, shape, dt=F32):
            return ctx.enter_context(nc.sbuf_tensor(name, shape, dt))

        def ps(name, shape, dt=F32):
            return ctx.enter_context(nc.psum_tensor(name, shape, dt))

        def sem(name):
            return ctx.enter_context(nc.semaphore(name))

        def dram(name, shape, dt=F32):
            return nc.dram_tensor(name, shape, dt, kind="Internal").ap()

        def bcast(v, n=P):
            return v.partition_broadcast(n)

        events = {}

        def event(name):
            if name not in events:
                events[name] = Event(sem("e_" + name))
            return events[name]

        def tile_of(a, t):
            return a[:, bass.ds(t, 1), :].rearrange("p a c -> p (a c)")

        def row_stats(c, v, st, mv, dif):
            c(v.tensor_tensor(mv[:, :, 0], st[:, :, 1], st[:, :, 4], ALU.add))
            c(v.tensor_scalar(mv[:, :, 0], mv[:, :, 0], 0.5, None, ALU.mult))
            c(v.tensor_tensor(dif, st[:, :, 1], mv[:, :, 0], ALU.subtract))
            c(v.tensor_tensor(dif, dif, dif, ALU.mult))
            c(v.tensor_tensor(mv[:, :, 1], st[:, :, 2], st[:, :, 5], ALU.add))
            c(v.scalar_tensor_tensor(out=mv[:, :, 1], in0=mv[:, :, 1], scalar=1.0 / D, in1=dif, op0=ALU.mult, op1=ALU.add))

        k_table = dram("k_table", (NP, D))
        v_table = dram("v_table", (NP, D))
        x3_table = dram("x3_table", (NP, D))
        y_table = dram("y_table", (YROWS, D))

        xall = sb("xall", [P, XT, D])
        mv = sb("mv", [P, XT, 2])
        rstd = sb("rstd", [P, XT])
        bn_st = sb("bn_st", [P, XT, 6])
        mdif = sb("mdif", [P, XT])
        ident = sb("ident", [P, P])
        ones = sb("ones", [P, P])
        iota_b = sb("iota_b", [P, P], BF16)
        identb = sb("identb", [P, P], BF16)
        iota_row = sb("iota_row", [P, P])
        iota_i = sb("iota_i", [P, P], I32)
        part = sb("part", [P, EQ])
        partk = sb("partk", [P, 4])
        iota_s = sb("iota_s", [P, 8], I32)

        w_qkv = sb("w_qkv", [P, KC, 3 * D])
        b_qkv = sb("b_qkv", [P, 3 * D])
        qe = sb("qe", [P, KC])
        qe01 = sb("qe01", [P, KC])
        rel = sb("rel", [R, HD])
        rel02 = sb("rel02", [R, HD])

        w_o = sb("w_o", [P, KC, D])
        b_o = sb("b_o", [1, D])
        gamma = sb("gamma", [P, D])
        beta = sb("beta", [P, D])
        gate_w = sb("gate_w", [P, KC, NX])
        gate_b = sb("gate_b", [1, NX])
        nmr = sb("nmr", [P, XT])
        be_i = sb("be_i", [P, BLOCKS], I32)
        slot_i = sb("slot_i", [P, BLOCKS], I32)
        pos_i = sb("pos_i", [P, NT, 2], I32)
        gates = sb("gates", [P, NT, 2])

        q_all = sb("q_all", [P, NT, D])
        src_idx = sb("src_idx", [P, STEPS], I32)
        dloc = sb("dloc", [P, STEPS + 2 * AHEAD])
        typ = sb("typ", [P, STEPS + 2 * AHEAD])
        dval = sb("dval", [P, STEPS])
        jk_i = sb("jk_i", [P, 2 + STEPS], I32)

        xn_st = sb("xn_st", [P, 2, D])
        enh_t = sb("enh_t", [P, 2, KC, P])
        k_all = sb("k_all", [P, NT, D + H])
        v_all = sb("v_all", [P, NT, D])

        table_ctx = ExitStack()

        def tb(name, shape, dt=F32):
            return table_ctx.enter_context(nc.sbuf_tensor(name, shape, dt))

        tab_i = tb("tab_i", [EP, 3, EQ, P], I32)
        tab_f = tb("tab_f", [EP, 3, EQ, P])
        cnt = tb("cnt", [EP, NT])
        junk = tb("junk", [EP, EQ * P])
        rowm = tb("rowm", [P, 8, NT])
        rowi = tb("rowi", [P, 2, NT], I32)
        cmp3 = tb("cmp3", [SP_, 3, 4, NODE_TILES])
        stepc = tb("stepc", [SP_, 3, 4])
        diag = tb("diag", [SP_, 2, 4, SP_])
        rows = tb("rows", [P, 2, STEPS])
        sel = tb("sel", [EP, EQ, STEPS])
        tmp_s = tb("tmp_s", [P, 3, STEPS])
        table_ctx.close()

        edge_ctx = ExitStack()

        def eb(name, shape, dt=F32):
            return edge_ctx.enter_context(nc.sbuf_tensor(name, shape, dt))

        idx_st = eb("idx_st", [P, GRP // STG, STG], I32)
        ring = eb("ring", [P, GRP, D])
        hot = eb("hot", [P, 4, 2, P + R], BF16)
        hot_n = eb("hot_n", [P, 2, 2, P])
        hot_r = eb("hot_r", [R, 2, 2, P])
        dif = eb("dif", [P, 2, 2, P + R], BF16)
        prod = eb("prod", [P, 2 * D])
        score = eb("score", [P, STEPS * H])

        scratch = q_all[:, :, :].rearrange("p t c -> p (t c)")

        def carve(at, n):
            return scratch[0:SP_, at * 2048:at * 2048 + n]

        sc_t = carve(0, 2048).rearrange("p (q h e) -> p q h e", q=4, h=H)
        fwd = carve(1, 2048).rearrange("p (q h e) -> p q h e", q=4, h=H)
        bwd = carve(2, 2048).rearrange("p (q h e) -> p q h e", q=4, h=H)
        wgt = eb("wgt", [P, STEPS * H])

        acc = k_all
        hotf = eb("hotf", [P, 4, 2, P])
        wv = eb("wv", [P, 2, 2, D + H])

        dst_t = eb("dst_t", [SP_, 4, P])
        brk_f = eb("brk_f", [SP_, 4, P])
        brk_b = eb("brk_b", [SP_, 4, P])
        ends = eb("ends", [SP_, 4, 4, H])
        end_rows = eb("end_rows", [H, 4, STEPS])
        link = eb("link", [H, 2, STEPS + 1])
        hop = eb("hop", [H, 2, STEPS])
        run = eb("run", [H, 2, STEPS + 2])
        carry = eb("carry", [SP_, 4, 2, H])

        edge_ctx.close()

        msg = sb("msg", [P, 2, D])
        msg_t = sb("msg_t", [P, 2, D])
        xnb = sb("xnb", [P, 2, D])
        zero = sb("zero", [P, NT, H])
        rden = sb("rden", [P, NT, H])
        st = sb("st", [P, XT, 6])
        mv2 = sb("mv2", [P, XT, 2])
        rs2 = sb("rs2", [P, XT])
        logits = sb("logits", [P, NT, NX])
        top = sb("top", [P, NT, 8])
        top_i = sb("top_i", [P, NT, 8], U32)
        top_f = sb("top_f", [P, NT, 2])
        oh = sb("oh", [P, 2, NT, NX])
        cm = sb("cm", [P, NT, NX])
        pre = sb("pre", [P, NT, NX])
        tot = sb("tot", [P, NT, NX])
        cinc = sb("cinc", [P, NT, NX])
        xrow = sb("xrow", [P, 6, NX])
        xrow_i = sb("xrow_i", [P, NX], I32)
        tok = sb("tok", [P, NT])
        tok_i = sb("tok_i", [P, NT], I32)
        vmask = sb("vmask", [P, NT])
        pos = sb("pos", [P, NT, 2])
        hi_i = sb("hi_i", [P, NT, 2], I32)
        lo_i = sb("lo_i", [P, NT, 2], I32)
        hi_f = sb("hi_f", [P, NT, 2])
        lo_f = sb("lo_f", [P, NT, 2])
        lo_hot = sb("lo_hot", [P, 2, P])
        hi_hot = sb("hi_hot", [P, 2, BLOCKS])
        beq = sb("beq", [P, BLOCKS, NX])
        bef = sb("bef", [P, BLOCKS])
        tri = sb("tri", [P, P])
        zeros = sb("zeros", [P, P])
        wx = [q_all[:, :, :].rearrange("p t c -> p (t c)")[:, i * 3072:(i + 1) * 3072] for i in range(2)]
        w12 = [w[:, 0:2048].rearrange("p (m c n) -> p m c n", m=2, c=KC) for w in wx]
        w3 = [w[:, 2048:3072].rearrange("p (c n) -> p c n", c=HC) for w in wx]
        slot_st = sb("slot_st", [P, 2, 1], I32)
        xg = sb("xg", [P, 2, D])
        xg_t = sb("xg_t", [P, 2, D])
        act1 = sb("act1", [P, 2, HID])
        hid = sb("hid", [P, 2, HID])
        hid_t = sb("hid_t", [P, 2, HID])
        y_st = sb("y_st", [P, 2, D])
        pos_st = sb("pos_st", [P, 4, 2], I32)
        yab = sb("yab", [P, 4, 2, D])
        x3_all = v_all
        x2_all = acc

        bank = [ps(f"bank{i}", [P, 512]) for i in range(8)]

        s_x, s_edges, s_w, s_b, s_rel = (sem(n) for n in ("s_x", "s_edges", "s_w", "s_b", "s_rel"))
        s_pool, s_dve, s_pe, s_act = (sem(n) for n in ("s_pool", "s_dve", "s_pe", "s_act"))
        s_stat = Stage(sem("s_stat"))
        s_xn, s_xt, s_enh, s_qk, s_vv, s_qcp, s_kcp, s_vcp = (
            Stage(sem(n)) for n in ("s_xn", "s_xt", "s_enh", "s_qk", "s_vv", "s_qcp", "s_kcp", "s_vcp"))
        s_kst = [sem("s_kst0"), sem("s_kst1")]
        s_vst = [sem("s_vst0"), sem("s_vst1")]
        a_idx, a_dif, a_hot, a_tr, a_ev, a_mm, a_add, a_prod, a_red = (
            Stage(sem(n)) for n in ("a_idx", "a_dif", "a_hot", "a_tr", "a_ev", "a_mm", "a_add", "a_prod", "a_red"))
        a_got = [sem(f"a_got{i}") for i in range(GRP)]
        m_t, m_ends, m_back, m_w = (event(n) for n in ("m_t", "m_ends", "m_back", "m_w"))
        b_idx, b_dif, b_hot, b_wv, b_wc, b_mm, b_acc = (
            Stage(sem(n), 2 * GRP) for n in ("b_idx", "b_dif", "b_hot", "b_wv", "b_wc", "b_mm", "b_acc"))
        b_got = [sem(f"b_got{i}") for i in range(GRP)]
        o_vz, o_xn, o_avg, o_msg, o_tr, o_ev, o_mm, o_sum, o_st, o_xb = (
            Stage(sem(n)) for n in ("o_vz", "o_xn", "o_avg", "o_msg", "o_tr", "o_ev", "o_mm", "o_sum", "o_st", "o_xb"))
        n_sc, n_ga, n_x2, n_st = (Stage(sem(n)) for n in ("n_sc", "n_ga", "n_x2", "n_st"))
        g_xn, g_tr, g_ev, g_mm, g_lg = (Stage(sem(n)) for n in ("g_xn", "g_tr", "g_ev", "g_mm", "g_lg"))
        r_hot, r_mm = Stage(sem("r_hot")), Stage(sem("r_mm"))
        f_st, f_tx, f_xt, f_h, f_si, f_hid, f_th, f_ht, f_y, f_yc = (
            Stage(sem(n)) for n in ("f_st", "f_tx", "f_xt", "f_h", "f_si", "f_hid", "f_th", "f_ht", "f_y", "f_yc"))
        s_w12 = [sem(f"s_w12{i}") for i in range(2)]
        s_w3 = [sem(f"s_w3{i}") for i in range(2)]
        s_xg = [sem(f"s_xg{i}") for i in range(2)]
        s_ys = [sem(f"s_ys{i}") for i in range(2)]
        c_st, c_a, c_o = Stage(sem("c_st")), Stage(sem("c_a")), Stage(sem("c_o"))
        s_ya = [sem(f"s_ya{i}") for i in range(8)]
        s_x3, s_w2, s_out = sem("s_x3"), sem("s_w2"), sem("s_out")
        s_pin = sem("s_pin")

        block = ctx.enter_context(nc.Block())

        @block.gpsimd
        def _(pool):
            c = Chain(pool, s_pool)
            c(pool.iota(iota_i[:, :], [[1, P]], base=0, channel_multiplier=0))
            c(pool.tensor_copy(iota_row[:, :], iota_i[:, :]))
            c(pool.iota(iota_s[:, 0:4], [[EP, 4]], base=0, channel_multiplier=1))
            c(pool.tensor_copy(part[:, :], iota_s[:, 0:4]))
            c(pool.iota(iota_s[:, 4:8], [[SP_, 4]], base=0, channel_multiplier=1))
            c(pool.tensor_copy(partk[:, :], iota_s[:, 4:8]))
            c(pool.memset(ones[:, :], 1.0))
            c(pool.memset(ident[:, :], 0.0))
            c(pool.affine_select(out=ident[:, :], in_=ident[:, :], compare_op=ALU.not_equal, fill=1.0, base=0,
                                 pattern=[[-1, P]], channel_multiplier=1))
            c(pool.tensor_copy(iota_b[:, :], iota_row[:, :]))
            c(pool.tensor_copy(identb[:, :], ident[:, :]))
            event("iota").set(pool)

            def gathers(table, got, staged, done):
                staged.open(pool)
                with pool.Fori(0, TURNS) as it:
                    for g in range(GRP // STG):
                        n = it * (GRP // STG) + g
                        done.hold(pool, n * (STG // 2) + (STG // 2 - 1) - PAIRS, s_pin)
                        pool.tensor_copy(idx_st[:, g, :], src_idx[:, bass.ds(it * GRP + g * STG, STG)]).then_inc(staged.sem, 1)
                        staged.hold(pool, n, s_pin)
                        for j in range(STG):
                            slot = g * STG + j
                            pool.indirect_dma_start(ring[:, slot, :], None, table, bass.IndirectOffsetOnAxis(ap=idx_st[:, g, j:j + 1], axis=0)).then_inc(got[slot], 16)

            event("tables").wait(pool)
            for b in range(2):
                pool.wait_ge(s_kst[b], 16 * (NT // 2))
            gathers(k_table, a_got, a_idx, a_prod)
            for b in range(2):
                pool.wait_ge(s_vst[b], 16 * (NT // 2))
            a_prod.wait(pool, TURNS * PAIRS - 1)
            gathers(v_table, b_got, b_idx, b_wv)

            o_vz.open(pool)
            o_xb.open(pool)
            event("zero").wait(pool)
            pool.wait_ge(s_w2, 96)
            with pool.Fori(0, NT) as t:
                a = tile_of(v_all, t).rearrange("p (h d) -> p h d", h=H)
                pool.tensor_tensor(a, a, tile_of(zero, t).unsqueeze(2).to_broadcast([P, H, HD]), ALU.mult).then_inc(o_vz.sem, 1)
            with pool.Fori(0, NT) as t:
                o_xn.hold(pool, t, s_pin)
                pool.tensor_tensor(tile_of(xall, t), tile_of(xall, t), beta[:, :], ALU.add).then_inc(o_xb.sem, 1)
            c(pool.iota(tok_i[:, :], [[P, NT]], base=0, channel_multiplier=1))
            c(pool.tensor_copy(tok[:, :], tok_i[:, :]))
            c(pool.memset(zeros[:, :], 0.0))
            c(pool.affine_select(out=tri[:, :], in_=ones[:, :], compare_op=ALU.is_gt, fill=0.0, base=0,
                                 pattern=[[1, P]], channel_multiplier=-1))
            event("tri").set(pool)

            f_st.open(pool)
            event("slots").wait(pool)
            pool.wait_ge(s_x3, 16 * NT)

            def gather_x(b, i):
                f_tx.hold(pool, b - 2, s_pin)
                pool.tensor_copy(slot_st[:, i, :], slot_i[:, bass.ds(b, 1)]).then_inc(f_st.sem, 1)
                f_st.hold(pool, b, s_pin)
                pool.indirect_dma_start(xg[:, i, :], None, x3_table, bass.IndirectOffsetOnAxis(ap=slot_st[:, i, :], axis=0)).then_inc(s_xg[i], 16)

            with pool.Fori(0, BLOCKS // 2) as it:
                for i in range(2):
                    gather_x(it * 2 + i, i)
            c_st.open(pool)
            for i in range(2):
                pool.wait_ge(s_ys[i], 16 * (BLOCKS // 2))
            with pool.Fori(0, NT // 2) as it:
                for i in range(2):
                    t = it * 2 + i
                    c_o.hold(pool, t - 2, s_pin)
                    pool.tensor_copy(pos_st[:, i, :], tile_of(pos_i, t)).then_inc(c_st.sem, 1)
                    c_st.hold(pool, t, s_pin)
                    for k in range(2):
                        pool.indirect_dma_start(yab[:, i, k, :], None, y_table, bass.IndirectOffsetOnAxis(ap=pos_st[:, i, k:k + 1], axis=0)).then_inc(s_ya[2 * i + k], 16)

        @block.vector
        def _(v):
            c = Chain(v, s_dve)
            for s in (s_stat, s_xn, s_qcp, s_kcp, s_vcp):
                s.open(v)
            v.wait_ge(s_edges, 48)
            c(v.tensor_copy(tab_f[:, :, :, :], tab_i[:, :, :, :]))
            c(v.memset(cnt[:, 0:1], 0.0))
            dst_f = tab_f[:, 1, :, :].rearrange("p q c -> p (q c)")
            for j in range(1, NT):
                c(v.tensor_scalar(junk[:, :], dst_f, float(P * j), 0.0, ALU.is_lt, ALU.add, accum_out=cnt[:, j:j + 1]))
            event("cnt").set(v)
            v.wait_ge(s_pe, 1)
            s_j, n_j, lo, hi, c_j, inc, exc, a_j = (rowm[:, i, 0:NODE_TILES] for i in range(8))
            c(v.tensor_copy(rowm[:, 0, :], bank[0][:, 0:NT]))
            s_next = rowm[:, 0, 1:NT]
            c(v.tensor_tensor(n_j, s_next, s_j, ALU.subtract))
            c(v.tensor_copy(rowi[:, 0, 0:NODE_TILES], s_j))
            c(v.tensor_scalar(rowi[:, 1, 0:NODE_TILES], s_next, -1.0, None, ALU.add))
            c(v.tensor_scalar(rowi[:, :, 0:NODE_TILES], rowi[:, :, 0:NODE_TILES], 7, None, ALU.arith_shift_right))
            c(v.tensor_copy(lo, rowi[:, 0, 0:NODE_TILES]))
            c(v.tensor_copy(hi, rowi[:, 1, 0:NODE_TILES]))
            c(v.tensor_tensor(hi, hi, lo, ALU.subtract))
            c(v.tensor_scalar(n_j, n_j, 0.0, None, ALU.is_gt))
            c(v.scalar_tensor_tensor(out=c_j, in0=hi, scalar=1.0, in1=n_j, op0=ALU.add, op1=ALU.mult))
            c(v.memset(n_j, 1.0))
            c(v.tensor_tensor_scan(inc, n_j, c_j, 0.0, ALU.mult, ALU.add))
            c(v.tensor_tensor(exc, inc, c_j, ALU.subtract))
            c(v.tensor_tensor(a_j, lo, exc, ALU.subtract))
            event("iota").wait(v)
            v3 = [SP_, 4, NODE_TILES]
            kk = partk[0:SP_, :].unsqueeze(2).to_broadcast(v3)
            for i, bound in enumerate((inc, exc)):
                c(v.tensor_tensor(cmp3[:, i, :, :], bound[0:SP_, :].unsqueeze(1).to_broadcast(v3), kk, ALU.is_le))
            c(v.tensor_reduce(stepc[:, 1, :], cmp3[:, 0, :, :], AX.X, ALU.add))
            c(v.tensor_tensor(cmp3[:, 2, :, :], cmp3[:, 1, :, :], cmp3[:, 0, :, :], ALU.subtract))
            c(v.tensor_tensor(cmp3[:, 2, :, :], cmp3[:, 2, :, :], a_j[0:SP_, :].unsqueeze(1).to_broadcast(v3), ALU.mult))
            c(v.tensor_reduce(stepc[:, 2, :], cmp3[:, 2, :, :], AX.X, ALU.add))
            c(v.tensor_tensor(stepc[:, 0, :], stepc[:, 2, :], partk[0:SP_, :], ALU.add))
            for i in range(2):
                for q in range(4):
                    c(v.tensor_scalar(diag[:, i, q, :], ident[0:SP_, 0:SP_], stepc[:, i, q:q + 1], None, ALU.mult))
            event("diag").set(v)
            v.wait_ge(s_pe, 2)
            for i in range(2):
                c(v.tensor_copy(rows[:, i, :], bank[2 + i][:, 0:STEPS]))
            c(v.memset(jk_i[:, 0:2], 0.0))
            c(v.tensor_copy(jk_i[:, 2:2 + STEPS], rows[:, 1, :]))
            for q in range(EQ):
                c(v.tensor_scalar(sel[:, q, :], rows[0:EP, 0, :], part[0:EP, q:q + 1], None, ALU.is_equal))
            event("sel").set(v)
            v.wait_ge(s_pe, 3)
            c(v.tensor_copy(src_idx[:, :], bank[4][:, 0:STEPS]))
            c(v.memset(dloc[:, STEPS:STEPS + 2 * AHEAD], -1.0))
            c(v.memset(typ[:, STEPS:STEPS + 2 * AHEAD], -1.0))
            c(v.tensor_copy(typ[:, 0:STEPS], bank[6][:, 0:STEPS]))
            c(v.scalar_tensor_tensor(out=dloc[:, 0:STEPS], in0=rows[:, 1, :], scalar=-float(P), in1=bank[5][:, 0:STEPS], op0=ALU.mult, op1=ALU.add))
            c(v.tensor_scalar(tmp_s[:, 0, :], dloc[:, 0:STEPS], 0.0, None, ALU.is_ge))
            c(v.tensor_scalar(tmp_s[:, 1, :], dloc[:, 0:STEPS], float(P), None, ALU.is_lt))
            c(v.tensor_tensor(tmp_s[:, 0, :], tmp_s[:, 0, :], tmp_s[:, 1, :], ALU.mult))
            c(v.scalar_tensor_tensor(out=tmp_s[:, 2, :], in0=bank[5][:, 0:STEPS], scalar=1.0, in1=tmp_s[:, 0, :], op0=ALU.add, op1=ALU.mult))
            c(v.tensor_scalar(dval[:, :], tmp_s[:, 2, :], -1.0, None, ALU.add))
            event("tables").set(v)

            v.wait_ge(s_x, 16)
            with v.Fori(0, XT) as t:
                v.bn_stats(tile_of(bn_st, t), tile_of(xall, t)).then_inc(s_stat.sem, 1)
            s_stat.wait(v, XT - 1)
            row_stats(c, v, bn_st, mv, mdif[:, :])
            c(v.tensor_scalar(rstd[:, :], mv[:, :, 1], EPS, None, ALU.add))
            event("var").set(v)
            v.wait_ge(s_act, 3)
            c(v.reciprocal(rstd[:, :], rstd[:, :]))
            c(v.scalar_tensor_tensor(out=nmr[:, :], in0=mv[:, :, 0], scalar=-1.0, in1=rstd[:, :], op0=ALU.mult, op1=ALU.mult))
            v.wait_ge(s_b, 64)
            def norm(t, b):
                s_xt.wait(v, t - 2)
                v.tensor_scalar(xn_st[:, b, :], tile_of(xall, t),
                                mv[:, bass.ds(t, 1), 0], rstd[:, bass.ds(t, 1)], ALU.subtract, ALU.mult).then_inc(s_xn.sem, 1)
            norm(0, 0)
            with v.Fori(0, NT // 2) as it:
                for b in range(2):
                    t = it * 2 + b
                    norm(t + 1, 1 - b)
                    s_qk.wait(v, t)
                    v.tensor_tensor(tile_of(q_all, t), bank[2 + b][:, 0:D], b_qkv[:, 0:D], ALU.add).then_inc(s_qcp.sem, 1)
                    v.tensor_tensor(tile_of(k_all, t)[:, 0:D], bank[2 + b][:, D:2 * D], b_qkv[:, D:2 * D], ALU.add).then_inc(s_kcp.sem, 1)
                    s_vv.wait(v, t)
                    v.tensor_tensor(tile_of(v_all, t), bank[4 + b][:, 0:D], b_qkv[:, 2 * D:3 * D], ALU.add).then_inc(s_vcp.sem, 1)
            s_qcp.wait(v, NT - 1)

            for s in (a_add, a_prod, a_red):
                s.open(v)

            with v.Fori(0, TURNS) as it:
                for i in range(PAIRS):
                    n, b = it * PAIRS + i, i % 2
                    rows2 = ring[:, 2 * i:2 * i + 2, :]
                    ring4 = rows2.rearrange("p u (h d) -> p u h d", h=H)
                    for u in range(2):
                        v.wait_ge(a_got[2 * i + u], it * 16 + 16)
                    a_mm.wait(v, n)
                    v.tensor_tensor(ring4, ring4, bank[4 + b][:, 0:2 * HD].rearrange("p (u d) -> p u d", u=2).unsqueeze(2).to_broadcast([P, 2, H, HD]), ALU.add).then_inc(a_add.sem, 1)
                    a_add.wait(v, n)
                    a_red.wait(v, n - 1)
                    v.tensor_tensor(prod[:, :], rows2.rearrange("p u c -> p (u c)"), bank[2 + b][:, :], ALU.mult).then_inc(a_prod.sem, 1)
                    a_prod.wait(v, n)
                    v.tensor_reduce(score[:, bass.ds(n * (2 * H), 2 * H)], prod[:, :].rearrange("p (g d) -> p g d", d=HD), AX.X, ALU.add).then_inc(a_red.sem, 1)
            a_red.wait(v, TURNS * PAIRS - 1)
            event("scores").set(v)

            m_t.wait(v)
            for q in range(4):
                c(v.tensor_copy(sc_t[:, q, :, :], bank[q][0:SP_, :].rearrange("p (h e) -> p h e", h=H)))
            c(v.tensor_copy(dst_t[:, :, :], bank[4][0:SP_, :].rearrange("p (q e) -> p q e", q=4)))
            c(v.memset(brk_f[:, :, 0:1], -BIG))
            c(v.memset(brk_b[:, :, P - 1:P], -BIG))
            c(v.tensor_tensor(brk_f[:, :, 1:P], dst_t[:, :, 1:P], dst_t[:, :, 0:P - 1], ALU.not_equal))
            c(v.tensor_scalar(brk_f[:, :, 1:P], brk_f[:, :, 1:P], -BIG, None, ALU.mult))
            c(v.tensor_copy(brk_b[:, :, 0:P - 1], brk_f[:, :, 1:P]))
            for q in range(4):
                for h in range(H):
                    v.tensor_tensor_scan(fwd[:, q, h, :], brk_f[:, q, :], sc_t[:, q, h, :], -BIG, ALU.add, ALU.max)
                    c(v.tensor_tensor_scan(bwd[:, q, h, ::-1], brk_b[:, q, ::-1], sc_t[:, q, h, ::-1], -BIG, ALU.add, ALU.max))
            c(v.tensor_copy(ends[:, :, 0, :], fwd[:, :, :, P - 1]))
            c(v.tensor_copy(ends[:, :, 1, :], bwd[:, :, :, 0]))
            c(v.tensor_copy(ends[:, :, 2, :], dst_t[:, :, 0:1].to_broadcast([SP_, 4, H])))
            c(v.tensor_copy(ends[:, :, 3, :], dst_t[:, :, P - 1:P].to_broadcast([SP_, 4, H])))
            event("ends").set(v)
            m_ends.wait(v)
            for i in range(4):
                c(v.tensor_copy(end_rows[:, i, :], bank[4 + i][0:H, 0:STEPS]))
            f_end, b_end, d_first, d_last = (end_rows[:, i, :] for i in range(4))
            c(v.memset(link[:, :, :], 0.0))
            c(v.tensor_tensor(link[:, 0, 1:STEPS], d_first[:, 1:STEPS], d_last[:, 0:STEPS - 1], ALU.is_equal))
            c(v.tensor_copy(link[:, 1, 0:STEPS - 1], link[:, 0, 1:STEPS]))
            c(v.tensor_tensor(hop[:, 0, :], d_first, d_last, ALU.is_equal))
            c(v.tensor_tensor(hop[:, 1, :], hop[:, 0, :], link[:, 1, 0:STEPS], ALU.mult))
            c(v.tensor_tensor(hop[:, 0, :], hop[:, 0, :], link[:, 0, 0:STEPS], ALU.mult))
            c(v.tensor_scalar(hop[:, :, :], hop[:, :, :], -1.0, BIG, ALU.add, ALU.mult))
            c(v.tensor_scalar(link[:, :, :], link[:, :, :], -1.0, BIG, ALU.add, ALU.mult))
            c(v.memset(run[:, :, :], -BIG))
            c(v.tensor_tensor_scan(run[:, 0, 1:STEPS + 1], hop[:, 0, :], f_end, -BIG, ALU.add, ALU.max))
            c(v.tensor_tensor_scan(run[:, 1, STEPS:0:-1], hop[:, 1, ::-1], b_end[:, ::-1], -BIG, ALU.add, ALU.max))
            c(v.tensor_tensor(hop[:, 0, :], run[:, 0, 0:STEPS], link[:, 0, 0:STEPS], ALU.add))
            c(v.tensor_tensor(hop[:, 1, :], run[:, 1, 2:STEPS + 2], link[:, 1, 0:STEPS], ALU.add))
            event("hop").set(v)
            m_back.wait(v)
            c(v.tensor_copy(carry[:, :, :, :], bank[4][0:SP_, 0:4 * 2 * H].rearrange("p (q i h) -> p q i h", q=4, i=2)))
            c(v.tensor_tensor(fwd, fwd, bwd, ALU.max))
            first = dst_t[:, :, 0:1].to_broadcast([SP_, 4, P])
            last = dst_t[:, :, P - 1:P].to_broadcast([SP_, 4, P])
            for i, (brk, edge) in enumerate(((brk_f, first), (brk_b, last))):
                c(v.tensor_tensor(brk[:, :, :], dst_t[:, :, :], edge, ALU.is_equal))
                c(v.tensor_scalar(brk[:, :, :], brk[:, :, :], -1.0, BIG, ALU.add, ALU.mult))
                for q in range(4):
                    for h in range(H):
                        ins = v.scalar_tensor_tensor(out=fwd[:, q, h, :], in0=brk[:, q, :], scalar=carry[:, q, i, h:h + 1],
                                                     in1=fwd[:, q, h, :], op0=ALU.add, op1=ALU.max)
                c(ins)
            c(v.tensor_tensor(sc_t, sc_t, fwd, ALU.subtract))
            event("diff").set(v)

            for s in (b_wv, b_acc):
                s.open(v)

            def weigh(it, i):
                n, b = it * PAIRS + i, i % 2
                for u in range(2):
                    v.wait_ge(b_got[2 * i + u], it * 16 + 16)
                b_mm.wait(v, n - 2)
                v.tensor_tensor(wv[:, b, :, 0:D].rearrange("p u (h d) -> p u h d", h=H),
                                ring[:, 2 * i:2 * i + 2, :].rearrange("p u (h d) -> p u h d", h=H),
                                wgt[:, bass.ds(n * (2 * H), 2 * H)].rearrange("p (u h) -> p u h", u=2).unsqueeze(3).to_broadcast([P, 2, H, HD]),
                                ALU.mult).then_inc(b_wv.sem, 1)

            for b in range(2):
                v.wait_ge(s_kst[b], 16 * (NT // 2))
            c(v.memset(acc[:, :, :], 0.0))
            event("acc_0").set(v)
            m_w.wait(v)
            event("primed").wait(v)

            def add(n, b, u):
                tile = v.value_load(jk_i[0:1, bass.ds(n * 2 + u, 1)], min_val=0, max_val=NT - 1)
                b_mm.wait(v, n - 1)
                b_acc.wait(v, n * 2 + (u - 1))
                a = tile_of(acc, tile)
                v.tensor_tensor(a, a, bank[2 * b + u][:, 0:D + H], ALU.add).then_inc(b_acc.sem, 1)

            with v.Fori(0, TURNS) as it:
                for i in range(PAIRS):
                    weigh(it, i)
                    for u in range(2):
                        add(it * PAIRS + i, 1 - i % 2, u)
            for u in range(2):
                add(TURNS * PAIRS, 1, u)
            b_acc.wait(v, STEPS + 1)

            for s in (o_avg, o_msg, o_sum, o_st):
                s.open(v)
            c(v.tensor_scalar(zero[:, :, :], acc[:, :, D:D + H], 0.0, None, ALU.is_equal))
            event("zero").set(v)
            c(v.tensor_tensor(rden[:, :, :], acc[:, :, D:D + H], zero[:, :, :], ALU.add))
            c(v.reciprocal(rden[:, :, :], rden[:, :, :]))
            with v.Fori(0, NT // 2) as it:
                for b in range(2):
                    t = it * 2 + b
                    o_tr.wait(v, t - 2)
                    v.tensor_tensor(msg[:, b, :].rearrange("p (h d) -> p h d", h=H), tile_of(acc, t)[:, 0:D].rearrange("p (h d) -> p h d", h=H),
                                    tile_of(rden, t).unsqueeze(2).to_broadcast([P, H, HD]), ALU.mult).then_inc(o_avg.sem, 1)
                    o_vz.wait(v, t)
                    o_avg.wait(v, t)
                    v.tensor_tensor(msg[:, b, :], msg[:, b, :], tile_of(v_all, t), ALU.add).then_inc(o_msg.sem, 1)
                for b in range(2):
                    t = it * 2 + b
                    o_mm.wait(v, t)
                    o_xn.wait(v, t)
                    a = tile_of(acc, t)[:, 0:D]
                    v.tensor_tensor(a, bank[2 + b][:, 0:D], xnb[:, b, :], ALU.add).then_inc(o_sum.sem, 1)
                    o_sum.wait(v, t)
                    v.bn_stats(tile_of(st, t), a).then_inc(o_st.sem, 1)
            o_st.wait(v, NT - 1)

            def norm_stats(name, sqrt_n):
                row_stats(c, v, st[:, 0:NT, :], mv2[:, 0:NT, :], mdif[:, 0:NT])
                c(v.tensor_scalar(rs2[:, 0:NT], mv2[:, 0:NT, 1], EPS, None, ALU.add))
                event(name).set(v)
                v.wait_ge(s_act, sqrt_n)
                c(v.reciprocal(rs2[:, 0:NT], rs2[:, 0:NT]))

            norm_stats("var2", 9)
            for s in (n_sc, n_ga, n_x2, n_st):
                s.open(v)
            with v.Fori(0, NT // 2) as it:
                for b in range(2):
                    t = it * 2 + b
                    a = tile_of(acc, t)[:, 0:D]
                    v.tensor_scalar(a, a, mv2[:, bass.ds(t, 1), 0], rs2[:, bass.ds(t, 1)], ALU.subtract, ALU.mult).then_inc(n_sc.sem, 1)
                for b in range(2):
                    t = it * 2 + b
                    a = tile_of(acc, t)[:, 0:D]
                    n_sc.wait(v, t)
                    v.tensor_tensor(a, a, gamma[:, :], ALU.mult).then_inc(n_ga.sem, 1)
                for b in range(2):
                    t = it * 2 + b
                    a = tile_of(acc, t)[:, 0:D]
                    n_ga.wait(v, t)
                    o_xb.wait(v, t)
                    v.tensor_tensor(a, a, tile_of(xall, t), ALU.add).then_inc(n_x2.sem, 1)
                for b in range(2):
                    t = it * 2 + b
                    n_x2.wait(v, t)
                    v.bn_stats(tile_of(st, t), tile_of(acc, t)[:, 0:D]).then_inc(n_st.sem, 1)
            n_st.wait(v, NT - 1)
            norm_stats("var3", 10)
            for s in (g_xn, g_lg):
                s.open(v)
            with v.Fori(0, NT // 2) as it:
                for b in range(2):
                    t = it * 2 + b
                    g_tr.wait(v, t - 2)
                    for to, stage in ((msg[:, b, :], o_msg), (tile_of(x3_all, t), g_xn)):
                        v.tensor_scalar(to, tile_of(x2_all, t)[:, 0:D], mv2[:, bass.ds(t, 1), 0], rs2[:, bass.ds(t, 1)], ALU.subtract, ALU.mult).then_inc(stage.sem, 1)
                for b in range(2):
                    t = it * 2 + b
                    g_mm.wait(v, t)
                    v.tensor_scalar(tile_of(logits, t), bank[2 + b][:, 0:NX], 1.0, None, ALU.mult).then_inc(g_lg.sem, 1)
            g_lg.wait(v, NT - 1)

            for t in range(NT):
                ins = v.max(top[:, t, :], logits[:, t, :])
            c(ins)
            for t in range(NT):
                ins = v.max_index(top_i[:, t, :], top[:, t, :], logits[:, t, :])
            c(ins)
            c(v.tensor_copy(top_f[:, :, :], top_i[:, :, 0:2]))
            c(v.tensor_tensor(gates[:, :, 1], top[:, :, 1], top[:, :, 0], ALU.subtract))
            event("dl").set(v)
            event("tri").wait(v)
            c(v.tensor_scalar(vmask[:, :], tok[:, :], float(N), None, ALU.is_lt))
            sh = [P, NT, NX]
            for k in range(2):
                c(v.tensor_tensor(oh[:, k, :, :], iota_row[:, 0:NX].unsqueeze(1).to_broadcast(sh), top_f[:, :, k:k + 1].to_broadcast(sh), ALU.is_equal))
                c(v.tensor_tensor(oh[:, k, :, :], oh[:, k, :, :], vmask[:, :].unsqueeze(2).to_broadcast(sh), ALU.mult))
            c(v.tensor_tensor(cm[:, :, :], oh[:, 0, :, :], oh[:, 1, :, :], ALU.add))
            event("cm").set(v)
            event("counts").wait(v)
            c(v.tensor_copy(pre[:, :, :], bank[0][:, 0:NT * NX].rearrange("p (t x) -> p t x", x=NX)))
            c(v.tensor_copy(tot[:, :, :], bank[1][:, 0:NT * NX].rearrange("p (t x) -> p t x", x=NX)))
            for x in range(NX):
                ins = v.tensor_tensor_scan(cinc[:, :, x], ones[:, 0:NT], tot[:, :, x], 0.0, ALU.mult, ALU.add)
            c(ins)
            x_cnt, x_nb, x_inc, x_base = (xrow[:, i, :] for i in range(4))
            c(v.tensor_scalar(x_cnt, cinc[:, NT - 1, :], float(P - 1), None, ALU.add))
            c(v.tensor_copy(xrow_i[:, :], x_cnt))
            c(v.tensor_scalar(xrow_i[:, :], xrow_i[:, :], 7, None, ALU.arith_shift_right))
            c(v.tensor_copy(x_nb, xrow_i[:, :]))
            c(v.tensor_tensor_scan(x_inc, ones[:, 0:NX], x_nb, 0.0, ALU.mult, ALU.add))
            c(v.tensor_tensor(x_base, x_inc, x_nb, ALU.subtract))
            c(v.tensor_scalar(x_base, x_base, float(P), None, ALU.mult))
            c(v.tensor_tensor(cinc[:, :, :], cinc[:, :, :], tot[:, :, :], ALU.subtract))
            c(v.tensor_tensor(cinc[:, :, :], cinc[:, :, :], pre[:, :, :], ALU.add))
            c(v.tensor_tensor(cinc[:, :, :], cinc[:, :, :], x_base.unsqueeze(1).to_broadcast(sh), ALU.add))
            for k in range(2):
                c(v.tensor_tensor(oh[:, k, :, :], oh[:, k, :, :], cinc[:, :, :], ALU.mult))
                c(v.tensor_reduce(pos[:, :, k], oh[:, k, :, :], AX.X, ALU.add))
            c(v.tensor_copy(pos_i[:, :, :], pos[:, :, :]))
            c(v.tensor_scalar(hi_i[:, :, :], pos_i[:, :, :], 7, None, ALU.arith_shift_right))
            c(v.tensor_scalar(lo_i[:, :, :], pos_i[:, :, :], P - 1, None, ALU.bitwise_and))
            c(v.tensor_copy(hi_f[:, :, :], hi_i[:, :, :]))
            c(v.tensor_copy(lo_f[:, :, :], lo_i[:, :, :]))
            c(v.tensor_scalar(vmask[:, :], vmask[:, :], -1.0, -float(4 * BLOCKS), ALU.add, ALU.mult))
            c(v.tensor_tensor(hi_f[:, :, :], hi_f[:, :, :], vmask[:, :].unsqueeze(2).to_broadcast([P, NT, 2]), ALU.add))
            sb_ = [P, BLOCKS, NX]
            c(v.tensor_tensor(beq[:, :, :], x_inc.unsqueeze(1).to_broadcast(sb_), iota_row[:, 0:BLOCKS].unsqueeze(2).to_broadcast(sb_), ALU.is_le))
            c(v.tensor_reduce(bef[:, :], beq[:, :, :], AX.X, ALU.add))
            c(v.tensor_scalar(be_i[:, :], bef[:, :], float(NX - 1), None, ALU.min))
            r_hot.open(v)
            with v.Fori(0, NODE_TILES) as t:
                for k in range(2):
                    n = t * 2 + k
                    r_mm.wait(v, n - 2)
                    v.tensor_scalar(lo_hot[:, k, :], iota_row[:, :], tile_of(lo_f, t)[:, k:k + 1], None, ALU.is_equal)
                    v.tensor_scalar(hi_hot[:, k, :], iota_row[:, 0:BLOCKS], tile_of(hi_f, t)[:, k:k + 1], tok[:, bass.ds(t, 1)], ALU.is_equal, ALU.mult).then_inc(r_hot.sem, 1)
            event("slot_sum").wait(v)
            c(v.tensor_copy(slot_i[:, :], bank[4][:, 0:BLOCKS]))
            event("slots").set(v)
            event("dexp").wait(v)
            c(v.tensor_scalar(gates[:, :, 0], gates[:, :, 1], 1.0, None, ALU.add))
            c(v.reciprocal(gates[:, :, 0], gates[:, :, 0]))
            c(v.tensor_tensor(gates[:, :, 1], gates[:, :, 1], gates[:, :, 0], ALU.mult))

            for s in (f_hid, f_yc):
                s.open(v)

            def gated(b, i):
                f_si.wait(v, b)
                f_th.wait(v, b - 2)
                v.tensor_tensor(hid[:, i, :], act1[:, i, :], bank[3 + i][:, :], ALU.mult).then_inc(f_hid.sem, 1)

            def take_y(b, i, first):
                f_y.wait(v, b)
                if not first:
                    v.wait_ge(s_ys[i], ys_done(b))
                v.tensor_copy(y_st[:, i, :], bank[6 + i][:, 0:D]).then_inc(f_yc.sem, 1)

            def ys_done(b):
                return (b // 2) * 16

            gated(0, 0)
            gated(1, 1)
            take_y(0, 0, True)
            gated(2, 0)
            take_y(1, 1, True)
            with v.Fori(0, (BLOCKS - 4) // 2) as it:
                for i in range(2):
                    gated(it * 2 + 3 + i, 1 - i)
                    f_y.wait(v, it * 2 + 2 + i)
                    v.wait_ge(s_ys[i], it * 16 + 16)
                    v.tensor_copy(y_st[:, i, :], bank[6 + i][:, 0:D]).then_inc(f_yc.sem, 1)
            gated(BLOCKS - 1, 1)
            for b in (BLOCKS - 2, BLOCKS - 1):
                take_y(b, b % 2, False)
            for s in (c_a, c_o):
                s.open(v)
            with v.Fori(0, NT // 2) as it:
                for k in range(2):
                    for i in range(2):
                        t = it * 2 + i
                        a = tile_of(x2_all, t)[:, 0:D]
                        v.wait_ge(s_ya[2 * i + k], it * 16 + 16)
                        if k:
                            c_a.wait(v, t)
                        v.scalar_tensor_tensor(out=a, in0=yab[:, i, k, :], scalar=tile_of(gates, t)[:, k:k + 1], in1=a,
                                               op0=ALU.mult, op1=ALU.add).then_inc((c_o if k else c_a).sem, 1)

        @block.sync
        def _(sp):
            for i, name in enumerate(("src", "dst", "typ")):
                sp.dma_start(tab_i[:, i, :, :], A[name].rearrange("(q p c) -> p q c", p=EP, c=P)).then_inc(s_edges, 16)
            sp.dma_start(xall[:, :, :], A["x"].rearrange("(t p) c -> p t c", p=P)).then_inc(s_x, 16)
            sp.dma_start(rel[:, :], A["rel_w"]).then_inc(s_rel, 16)
            with sp.Fori(0, NT // 2) as it:
                for b in range(2):
                    t = sp.snap(it * 2 + b)
                    row = sp.snap(t * P)
                    s_kcp.hold(sp, t, s_pin)
                    sp.dma_start(k_table[bass.ds(row, P), :], tile_of(k_all, t)[:, 0:D]).then_inc(s_kst[b], 16)
                    s_vcp.hold(sp, t, s_pin)
                    sp.dma_start(v_table[bass.ds(row, P), :], tile_of(v_all, t)).then_inc(s_vst[b], 16)
            with sp.Fori(0, NT) as t:
                row = sp.snap(t * P)
                g_xn.hold(sp, t, s_pin)
                sp.dma_start(x3_table[bass.ds(row, P), :], tile_of(x3_all, t)).then_inc(s_x3, 16)
            event("slots").wait(sp)

            def load_w12(b, i):
                e = sp.value_load(be_i[0:1, bass.ds(b, 1)], min_val=0, max_val=NX - 1)
                f_h.hold(sp, b - 2, s_pin)
                for m, w in enumerate(("w1", "w2")):
                    sp.dma_start(w12[i][:, m, :, :], A[w][bass.ds(e, 1), :, :].rearrange("e (c p) n -> p (e c) n", p=P)).then_inc(s_w12[i], 16)

            def load_w3(b, i):
                e = sp.value_load(be_i[0:1, bass.ds(b, 1)], min_val=0, max_val=NX - 1)
                f_y.hold(sp, b - 2, s_pin)
                sp.dma_start(w3[i], A["w3"][bass.ds(e, 1), :, :].rearrange("e (c p) n -> p (e c) n", p=P)).then_inc(s_w3[i], 16)

            def store_y(b, i):
                row = sp.snap(b * P)
                f_yc.hold(sp, b, s_pin)
                sp.dma_start(y_table[bass.ds(row, P), :], y_st[:, i, :]).then_inc(s_ys[i], 16)

            for b in range(2):
                load_w12(b, b)
                load_w3(b, b)
            with sp.Fori(0, BLOCKS // 2 - 1) as it:
                for i in range(2):
                    b = it * 2 + i
                    load_w12(b + 2, i)
                    store_y(b, i)
                    load_w3(b + 2, i)
            for i in range(2):
                store_y(BLOCKS - 2 + i, i)
            with sp.Fori(0, NT) as t:
                row = sp.snap(t * P)
                c_o.hold(sp, t, s_pin)
                sp.dma_start(out[bass.ds(row, P), :], tile_of(x2_all, t)[:, 0:D]).then_inc(s_out, 16)
            sp.wait_ge(s_out, 16 * NT)

        @block.scalar
        def _(act):
            for i, n in enumerate(("Wq", "Wk", "Wv")):
                act.dma_start(w_qkv[:, :, i * D:(i + 1) * D], A[n].rearrange("(c p) n -> p c n", p=P)).then_inc(s_w, 16)
            for i, n in enumerate(("bq", "bk", "bv")):
                act.dma_start(b_qkv[:, i * D:(i + 1) * D], bcast(A[n])).then_inc(s_b, 16)
            act.dma_start(qe[:, :], A["query_emb"].rearrange("(c p) -> p c", p=P), allow_slow_non_contiguous=True).then_inc(s_b, 16)
            act.dma_start(w_o[:, :, :], A["Wo"].rearrange("(c p) n -> p c n", p=P)).then_inc(s_w2, 16)
            act.dma_start(gate_w[:, :, :], A["gate_w"].rearrange("(c p) n -> p c n", p=P)).then_inc(s_w2, 16)
            act.dma_start(gamma[:, :], bcast(A["gamma"])).then_inc(s_w2, 16)
            act.dma_start(beta[:, :], bcast(A["beta"])).then_inc(s_w2, 16)
            act.dma_start(b_o[:, :], A["bo"].rearrange("(a n) -> a n", a=1)).then_inc(s_w2, 16)
            act.dma_start(gate_b[:, :], A["gate_b"].rearrange("(a n) -> a n", a=1)).then_inc(s_w2, 16)
            act.wait_ge(s_b, 64)
            act.wait_ge(s_rel, 16)
            act.activation(qe01[:, :], qe[:, :], ACT.Copy, scale=0.1).then_inc(s_act, 1)
            act.activation(rel02[:, :], rel[:, :], ACT.Copy, scale=0.2).then_inc(s_act, 1)
            event("var").wait(act)
            act.activation(rstd[:, :], rstd[:, :], ACT.Sqrt).then_inc(s_act, 1)
            act.wait_ge(s_act, 2)
            s_enh.open(act)
            with act.Fori(0, NT // 2) as it:
                for b in range(2):
                    t = it * 2 + b
                    s_qk.wait(act, t - 2)
                    s_xt.wait(act, t)
                    for c in range(KC):
                        ins = act.activation(enh_t[:, b, c, :], bank[b][:, c * P:(c + 1) * P], ACT.Identity,
                                             bias=qe01[:, c:c + 1])
                    ins.then_inc(s_enh.sem, 1)

            for s in (a_dif, a_hot, a_ev):
                s.open(act)

            def hot_dif(n, b):
                for u in range(2):
                    act.activation(dif[:, b, u, 0:P], iota_b[:, :], ACT.Abs, bias=dloc[:, bass.ds(n * 2 + u, 1)], scale=-1.0)
                    ins = act.activation(dif[:, b, u, P:P + R], iota_b[:, 0:R], ACT.Abs, bias=typ[:, bass.ds(n * 2 + u, 1)], scale=-1.0)
                ins.then_inc(a_dif.sem, 1)

            def hot_relu(n, b, hb):
                a_dif.wait(act, n)
                a_tr.wait(act, n - 4)
                act.activation(hot[:, hb, :, :], dif[:, b, :, :], ACT.Relu, bias=ones[:, 0:1], scale=-1.0).then_inc(a_hot.sem, 1)

            event("tables").wait(act)
            for n in range(AHEAD):
                hot_dif(n, n % 2)
                hot_relu(n, n % 2, n)
            with act.Fori(0, TURNS) as it:
                for i in range(PAIRS):
                    n, b = it * PAIRS + i, i % 2
                    hot_dif(n + AHEAD, (i + AHEAD) % 2)
                    a_mm.wait(act, n - 2)
                    a_tr.wait(act, n)
                    t = bank[b][:, :].bitcast(BF16)[:, 0:4 * P].rearrange("p (u x) -> p u x", u=2)
                    act.activation(hot_n[:, b, :, :], t[:, :, 0:P], ACT.Copy)
                    act.activation(hot_r[:, b, :, :], t[0:R, :, P:2 * P], ACT.Copy).then_inc(a_ev.sem, 1)
                    hot_relu(n + AHEAD, (i + AHEAD) % 2, (i + AHEAD) % 4)
            event("diff").wait(act)
            act.activation(sc_t, sc_t, ACT.Exp, scale=HD ** -0.5).then_inc(s_act, 1)
            act.wait_ge(s_act, 4)
            event("exp").set(act)
            event("w_t").wait(act)
            wgt4 = wgt[:, :].rearrange("p (q k h) -> p q h k", q=4, h=H)
            for q in range(4):
                act.activation(wgt4[:, q, :, :], bank[q][:, 0:H * SP_].rearrange("p (h k) -> p h k", h=H), ACT.Copy).then_inc(s_act, 1)
            act.wait_ge(s_act, 8)
            m_w.set(act)
            for s in (b_dif, b_hot, b_wc):
                s.open(act)

            def hotf_dif(n, b):
                for u in range(2):
                    ins = act.activation(dif[:, b, u, 0:P], iota_b[:, :], ACT.Abs, bias=dloc[:, bass.ds(n * 2 + u, 1)], scale=-1.0)
                ins.then_inc(b_dif.sem, 1)

            def hotf_relu(n, b, hb):
                b_dif.wait(act, n)
                b_mm.wait(act, n - 4)
                act.activation(hotf[:, hb, :, :], dif[:, b, :, 0:P], ACT.Relu, bias=ones[:, 0:1], scale=-1.0).then_inc(b_hot.sem, 1)

            for n in range(AHEAD):
                hotf_dif(n, n % 2)
                hotf_relu(n, n % 2, n)
            with act.Fori(0, TURNS) as it:
                for i in range(PAIRS):
                    n, b = it * PAIRS + i, i % 2
                    hotf_dif(n + AHEAD, (i + AHEAD) % 2)
                    b_mm.wait(act, n - 2)
                    act.activation(wv[:, b, :, D:D + H], wgt[:, bass.ds(n * (2 * H), 2 * H)].rearrange("p (u h) -> p u h", u=2), ACT.Copy).then_inc(b_wc.sem, 1)
                    hotf_relu(n + AHEAD, (i + AHEAD) % 2, (i + AHEAD) % 4)
            o_xn.open(act)
            o_ev.open(act)
            act.wait_ge(s_w2, 96)
            with act.Fori(0, NT // 2) as it:
                for b in range(2):
                    t = it * 2 + b
                    o_sum.wait(act, t - 2)
                    act.activation(xnb[:, b, :], tile_of(xall, t), ACT.Identity, bias=nmr[:, bass.ds(t, 1)], scale=rstd[:, bass.ds(t, 1)]).then_inc(o_xn.sem, 1)
                    o_tr.wait(act, t)
                    o_mm.wait(act, t - 2)
                    act.activation(msg_t[:, b, :], bank[b][:, 0:D], ACT.Copy).then_inc(o_ev.sem, 1)
            for i, name in enumerate(("var2", "var3")):
                event(name).wait(act)
                act.activation(rs2[:, 0:NT], rs2[:, 0:NT], ACT.Sqrt).then_inc(s_act, 1)
            g_ev.open(act)
            with act.Fori(0, NT // 2) as it:
                for b in range(2):
                    t = it * 2 + b
                    g_tr.wait(act, t)
                    g_mm.wait(act, t - 2)
                    act.activation(msg_t[:, b, :], bank[b][:, 0:D], ACT.Copy).then_inc(g_ev.sem, 1)
            event("dl").wait(act)
            act.activation(gates[:, :, 1], gates[:, :, 1], ACT.Exp).then_inc(s_act, 1)
            act.wait_ge(s_act, 11)
            event("dexp").set(act)
            for s in (f_xt, f_si, f_ht):
                s.open(act)

            def copy_xt(b, i):
                f_tx.wait(act, b)
                f_h.wait(act, b - 2)
                act.activation(xg_t[:, i, :], bank[0][:, 0:D], ACT.Copy).then_inc(f_xt.sem, 1)

            def silu(b, i):
                f_h.wait(act, b)
                f_hid.wait(act, b - 2)
                act.activation(act1[:, i, :], bank[1 + i][:, :], ACT.Silu).then_inc(f_si.sem, 1)

            def copy_ht(b, i):
                f_th.wait(act, b)
                f_y.wait(act, b - 2)
                act.activation(hid_t[:, i, :], bank[5][:, :], ACT.Copy).then_inc(f_ht.sem, 1)

            copy_xt(0, 0)
            silu(0, 0)
            copy_xt(1, 1)
            with act.Fori(0, BLOCKS // 2 - 1) as it:
                for i in range(2):
                    b = it * 2 + 1 + i
                    copy_ht(b - 1, i)
                    silu(b, 1 - i)
                    copy_xt(b + 1, i)
            copy_ht(BLOCKS - 2, 0)
            silu(BLOCKS - 1, 1)
            copy_ht(BLOCKS - 1, 1)

        @block.tensor
        def _(pe):
            s_xt.open(pe)
            s_qk.open(pe)
            s_vv.open(pe)
            event("iota").wait(pe)
            event("cnt").wait(pe)
            pe.matmul(bank[0][:, 0:NT], ones[0:EP, :], cnt[:, :], start=True, stop=True).then_inc(s_pe, 1)
            event("diag").wait(pe)
            for v in range(2):
                for q in range(4):
                    ins = pe.matmul(bank[2 + v][:, q * SP_:(q + 1) * SP_], ones[0:SP_, :], diag[:, v, q, :],
                                    start=True, stop=True)
            ins.then_inc(s_pe, 1)
            event("sel").wait(pe)
            for i in range(3):
                for q in range(EQ):
                    ins = pe.matmul(bank[4 + i][:, 0:STEPS], tab_f[:, i, q, :], sel[:, q, :], start=(q == 0), stop=(q == EQ - 1))
            ins.then_inc(s_pe, 1)
            pe.wait_ge(s_w, 48)
            def transposes(t, b):
                s_xn.wait(pe, t)
                s_enh.wait(pe, t - 2)
                for c in range(KC):
                    ins = pe.transpose(bank[b][:, c * P:(c + 1) * P], xn_st[:, b, c * P:(c + 1) * P], ident[:, :])
                ins.then_inc(s_xt.sem, 1)
            with pe.Fori(0, NT // 2) as it:
                for b in range(2):
                    t = it * 2 + b
                    transposes(t, b)
                    s_enh.wait(pe, t)
                    s_kcp.wait(pe, t - 2)
                    for c in range(KC):
                        ins = pe.matmul(bank[2 + b][:, :], enh_t[:, b, c, :], w_qkv[:, c, 0:2 * D], start=(c == 0), stop=(c == KC - 1))
                    ins.then_inc(s_qk.sem, 1)
                    s_vcp.wait(pe, t - 2)
                    for c in range(KC):
                        ins = pe.matmul(bank[4 + b][:, 0:D], enh_t[:, b, c, :], w_qkv[:, c, 2 * D:3 * D], start=(c == 0), stop=(c == KC - 1))
                    ins.then_inc(s_vv.sem, 1)

            a_tr.open(pe)
            a_mm.open(pe)

            def hot_transposes(n, b, hb):
                a_hot.wait(pe, n)
                a_ev.wait(pe, n - 2)
                t = bank[b][:, :].bitcast(BF16)
                for u in range(2):
                    pe.transpose(t[:, 2 * u * P:(2 * u + 1) * P], hot[:, hb, u, 0:P], identb[:, :])
                    ins = pe.transpose(t[0:R, (2 * u + 1) * P:(2 * u + 2) * P], hot[:, hb, u, P:P + R], identb[:, :])
                ins.then_inc(a_tr.sem, 1)

            s_vcp.wait(pe, NT - 1)
            hot_transposes(0, 0, 0)
            with pe.Fori(0, TURNS) as it:
                for i in range(PAIRS):
                    n, b = it * PAIRS + i, i % 2
                    tiles = [pe.value_load(jk_i[0:1, bass.ds(n * 2 + u + 2, 1)], min_val=0, max_val=NT - 1) for u in range(2)]
                    hot_transposes(n + 1, 1 - b, (i + 1) % 4)
                    a_ev.wait(pe, n)
                    a_prod.wait(pe, n - 2)
                    for u in range(2):
                        pe.matmul(bank[2 + b][:, u * D:(u + 1) * D], hot_n[:, b, u, :], tile_of(q_all, tiles[u]), start=True, stop=True)
                        ins = pe.matmul(bank[4 + b][:, u * HD:(u + 1) * HD], hot_r[:, b, u, :], rel02[:, :], start=True, stop=True)
                    ins.then_inc(a_mm.sem, 1)

            def done(ins, what):
                pe_n[0] += 1
                ins.then_inc(s_pe, 1)
                pe.wait_ge(s_pe, pe_n[0])
                what.set(pe)

            pe_n = [3]
            event("scores").wait(pe)
            score4 = score[:, :].rearrange("p (q k h) -> p q h k", q=4, h=H)
            for q in range(4):
                for h in range(H):
                    pe.transpose(bank[q][0:SP_, h * P:(h + 1) * P], score4[:, q, h, :], ident[:, :])
                ins = pe.transpose(bank[4][0:SP_, q * P:(q + 1) * P], dval[:, q * SP_:(q + 1) * SP_], ident[:, :])
            done(ins, m_t)
            event("ends").wait(pe)
            for i in range(4):
                for q in range(4):
                    ins = pe.transpose(bank[4 + i][0:H, q * SP_:(q + 1) * SP_], ends[:, q, i, :], ident[0:SP_, 0:SP_])
            done(ins, m_ends)
            event("hop").wait(pe)
            for q in range(4):
                for i in range(2):
                    ins = pe.transpose(bank[4][0:SP_, (q * 2 + i) * H:(q * 2 + i + 1) * H], hop[:, i, q * SP_:(q + 1) * SP_], ident[0:H, 0:H])
            done(ins, m_back)
            event("exp").wait(pe)
            for q in range(4):
                for h in range(H):
                    ins = pe.transpose(bank[q][:, h * SP_:(h + 1) * SP_], sc_t[:, q, h, :], ident[0:SP_, 0:SP_])
            done(ins, event("w_t"))

            b_mm.open(pe)
            m_w.wait(pe)
            event("acc_0").wait(pe)
            for u in range(2):
                ins = pe.matmul(bank[2 + u][:, 0:D + H], acc[:, 0, 0:P], acc[:, 1, :], start=True, stop=True)
            done(ins, event("primed"))
            with pe.Fori(0, TURNS) as it:
                for i in range(PAIRS):
                    n, b = it * PAIRS + i, i % 2
                    b_hot.wait(pe, n)
                    b_wv.wait(pe, n)
                    b_wc.wait(pe, n)
                    b_acc.wait(pe, n * 2 - 1)
                    for u in range(2):
                        ins = pe.matmul(bank[2 * b + u][:, 0:D + H], hotf[:, i % 4, u, :], wv[:, b, u, :], start=True, stop=True)
                    ins.then_inc(b_mm.sem, 1)

            o_tr.open(pe)
            o_mm.open(pe)
            pe.wait_ge(s_w2, 96)
            b_acc.wait(pe, STEPS + 1)
            with pe.Fori(0, NT // 2) as it:
                for b in range(2):
                    t = it * 2 + b
                    o_msg.wait(pe, t)
                    o_ev.wait(pe, t - 2)
                    for c in range(KC):
                        ins = pe.transpose(bank[b][:, c * P:(c + 1) * P], msg[:, b, c * P:(c + 1) * P], ident[:, :])
                    ins.then_inc(o_tr.sem, 1)
                for b in range(2):
                    t = it * 2 + b
                    o_ev.wait(pe, t)
                    o_sum.wait(pe, t - 2)
                    for c in range(KC):
                        pe.matmul(bank[2 + b][:, 0:D], msg_t[:, b, c * P:(c + 1) * P], w_o[:, c, :], start=(c == 0), stop=False)
                    pe.matmul(bank[2 + b][:, 0:D], ones[0:1, :], b_o[:, :], start=False, stop=True).then_inc(o_mm.sem, 1)
            g_tr.open(pe)
            g_mm.open(pe)
            with pe.Fori(0, NT // 2) as it:
                for b in range(2):
                    t = it * 2 + b
                    o_msg.wait(pe, t + NT)
                    g_ev.wait(pe, t - 2)
                    for c in range(KC):
                        ins = pe.transpose(bank[b][:, c * P:(c + 1) * P], msg[:, b, c * P:(c + 1) * P], ident[:, :])
                    ins.then_inc(g_tr.sem, 1)
                for b in range(2):
                    t = it * 2 + b
                    g_ev.wait(pe, t)
                    g_lg.wait(pe, t - 2)
                    for c in range(KC):
                        pe.matmul(bank[2 + b][:, 0:NX], msg_t[:, b, c * P:(c + 1) * P], gate_w[:, c, :], start=(c == 0), stop=False)
                    pe.matmul(bank[2 + b][:, 0:NX], ones[0:1, :], gate_b[:, :], start=False, stop=True).then_inc(g_mm.sem, 1)
            event("cm").wait(pe)
            cmf = cm[:, :, :].rearrange("p t x -> p (t x)")
            pe.matmul(bank[0][:, 0:NT * NX], tri[:, :], cmf, start=True, stop=True)
            done(pe.matmul(bank[1][:, 0:NT * NX], ones[:, :], cmf, start=True, stop=True), event("counts"))
            r_mm.open(pe)
            slots = bank[4][:, 0:BLOCKS]
            pe.matmul(slots, zeros[:, :], zeros[:, 0:BLOCKS], start=True, stop=False)
            with pe.Fori(0, NODE_TILES) as t:
                for k in range(2):
                    r_hot.wait(pe, t * 2 + k)
                    pe.matmul(slots, lo_hot[:, k, :], hi_hot[:, k, :], start=False, stop=False).then_inc(r_mm.sem, 1)
            done(pe.matmul(slots, zeros[:, :], zeros[:, 0:BLOCKS], start=False, stop=True), event("slot_sum"))

            for s in (f_tx, f_h, f_th, f_y):
                s.open(pe)
            event("slots").wait(pe)

            def turn_x(b, i, got):
                pe.wait_ge(s_xg[i], got)
                f_xt.wait(pe, b - 1)
                for c in range(KC):
                    ins = pe.transpose(bank[0][:, c * P:(c + 1) * P], xg[:, i, c * P:(c + 1) * P], ident[:, :])
                ins.then_inc(f_tx.sem, 1)

            def first_half(b, i, got):
                f_xt.wait(pe, b)
                f_hid.wait(pe, b - 2)
                pe.wait_ge(s_w12[i], got)
                for m in range(2):
                    for c in range(KC):
                        ins = pe.matmul(bank[1 + 2 * m + i][:, :], xg_t[:, i, c * P:(c + 1) * P], w12[i][:, m, c, :], start=(c == 0), stop=(c == KC - 1))
                ins.then_inc(f_h.sem, 1)

            def turn_hid(b, i):
                f_hid.wait(pe, b)
                f_ht.wait(pe, b - 1)
                for c in range(HC):
                    ins = pe.transpose(bank[5][:, c * P:(c + 1) * P], hid[:, i, c * P:(c + 1) * P], ident[:, :])
                ins.then_inc(f_th.sem, 1)

            def second_half(b, i, got):
                f_ht.wait(pe, b)
                f_yc.wait(pe, b - 2)
                pe.wait_ge(s_w3[i], got)
                for c in range(HC):
                    ins = pe.matmul(bank[6 + i][:, 0:D], hid_t[:, i, c * P:(c + 1) * P], w3[i][:, c, :], start=(c == 0), stop=(c == HC - 1))
                ins.then_inc(f_y.sem, 1)

            turn_x(0, 0, 16)
            first_half(0, 0, 32)
            turn_x(1, 1, 16)
            with pe.Fori(0, BLOCKS // 2 - 1) as it:
                for i in range(2):
                    b = it * 2 + 1 + i
                    turn_hid(b - 1, i)
                    first_half(b, 1 - i, it * 32 + 32 * (1 + i))
                    second_half(b - 1, i, it * 16 + 16)
                    turn_x(b + 1, i, it * 16 + 32)
            turn_hid(BLOCKS - 2, 0)
            first_half(BLOCKS - 1, 1, 32 * (BLOCKS // 2))
            second_half(BLOCKS - 2, 0, 16 * (BLOCKS // 2))
            turn_hid(BLOCKS - 1, 1)
            second_half(BLOCKS - 1, 1, 16 * (BLOCKS // 2))


_INS = {"x": "x", "src": "src", "dst": "dst", "typ": "edge_type_64", "query_emb": "L0_gnn_query_emb",
        "Wq": "L0_gnn_Wq", "bq": "L0_gnn_bq", "Wk": "L0_gnn_Wk", "bk": "L0_gnn_bk", "Wv": "L0_gnn_Wv", "bv": "L0_gnn_bv",
        "rel_w": "L0_gnn_rel_w", "Wo": "L0_gnn_Wo", "bo": "L0_gnn_bo", "gamma": "L0_gnn_gamma", "beta": "L0_gnn_beta",
        "gate_w": "L0_ffn_gate_w", "gate_b": "L0_ffn_gate_b", "w1": "L0_ffn_w1", "w2": "L0_ffn_w2", "w3": "L0_ffn_w3"}



def kernel(**inputs):
    import numpy as np
    import concourse.bacc as bacc
    from concourse.bass_utils import run_bass_kernel_spmd as run

    nc = bacc.Bacc("TRN2", target_bir_lowering=False, num_devices=1)
    pads = {"x": (XT * P, 0), "src": (ET * P, 0), "dst": (ET * P, NO_DST), "typ": (ET * P, 0)}
    arrays, A = {}, {}
    for name, given in _INS.items():
        a = np.ascontiguousarray(inputs[given])
        if name in pads:
            rows, fill = pads[name]
            padded = np.full((rows,) + a.shape[1:], fill, a.dtype)
            padded[:a.shape[0]] = a
            a = padded
        arrays[f"in_{name}"] = a
        A[name] = nc.dram_tensor(f"in_{name}", a.shape, mybir.dt.from_np(a.dtype), kind="ExternalInput").ap()
    out = nc.dram_tensor("out_0", (NP, D), F32, kind="ExternalOutput").ap()
    build(nc, A, out)
    r = run(nc, [arrays], core_ids=[0])
    return r.results[0]["out_0"][:N]
```

```python
from contextlib import ExitStack

import concourse.bass as bass
from concourse import mybir

F32 = mybir.dt.float32
BF16 = mybir.dt.bfloat16
I32 = mybir.dt.int32
U32 = mybir.dt.uint32
ALU = mybir.AluOpType
ACT = mybir.ActivationFunctionType
AX = mybir.AxisListType

P = 128
N = 3125
D = 256
H = 4
HD = 64
R = 64
E = 50000
NX = 16
HID = 512
KC = D // P
HC = HID // P
NODE_TILES = -(-N // P)
NT = NODE_TILES + 1
NP = NT * P
XT = NT + 1
EP = 98
EQ = 4
ET = EP * EQ
SP_ = 104
STEPS = SP_ * 4
SLOT_TILES = 5
assert -(-E // P) + NODE_TILES - 1 <= STEPS and ET * P >= E
NO_DST = 1 << 20
BIG = 1.0e30
EPS = 1e-5
GRP = 16
STG = 8
AHEAD = 3
PAIRS = GRP // 2
TURNS = STEPS // GRP
BLOCKS = (2 * N + NX * (P - 1)) // P
YROWS = BLOCKS * P
WX = 2 * KC * HID + HC * D
WB = 4
CT = NT // 2
assert NODE_TILES % SLOT_TILES == 0 and NT % CT == 0


class Stage:

    def __init__(self, sem, credit=8):
        self.sem, self.credit = sem, credit

    def hold(self, eng, n, pin):
        self.wait(eng, n)
        eng.sem_inc(pin, 1)

    def open(self, eng):
        eng.sem_inc(self.sem, self.credit)

    def wait(self, eng, n):
        eng.wait_ge(self.sem, n + (1 + self.credit))


class Event:

    def __init__(self, sem):
        self.sem = sem

    def set(self, eng):
        eng.sem_inc(self.sem, 1)

    def wait(self, eng):
        eng.wait_ge(self.sem, 1)


class Chain:

    def __init__(self, eng, sem):
        self.eng, self.sem, self.n = eng, sem, 0

    def __call__(self, ins):
        self.n += 1
        ins.then_inc(self.sem, 1)
        self.eng.wait_ge(self.sem, self.n)


def build(nc, A, out):
    ctx = ExitStack()
    with ctx:
        def sb(name, shape, dt=F32):
            return ctx.enter_context(nc.sbuf_tensor(name, shape, dt))

        def ps(name, shape, dt=F32):
            return ctx.enter_context(nc.psum_tensor(name, shape, dt))

        def sem(name):
            return ctx.enter_context(nc.semaphore(name))

        def dram(name, shape, dt=F32):
            return nc.dram_tensor(name, shape, dt, kind="Internal").ap()

        def bcast(v, n=P):
            return v.partition_broadcast(n)

        events = {}

        def event(name):
            if name not in events:
                events[name] = Event(sem("e_" + name))
            return events[name]

        def tile_of(a, t):
            return a[:, bass.ds(t, 1), :].rearrange("p a c -> p (a c)")

        def row_stats(c, v, st, mv, dif):
            c(v.tensor_tensor(mv[:, :, 0], st[:, :, 1], st[:, :, 4], ALU.add))
            c(v.tensor_scalar(mv[:, :, 0], mv[:, :, 0], 0.5, None, ALU.mult))
            c(v.tensor_tensor(dif, st[:, :, 1], mv[:, :, 0], ALU.subtract))
            c(v.tensor_tensor(dif, dif, dif, ALU.mult))
            c(v.tensor_tensor(mv[:, :, 1], st[:, :, 2], st[:, :, 5], ALU.add))
            c(v.scalar_tensor_tensor(out=mv[:, :, 1], in0=mv[:, :, 1], scalar=1.0 / D, in1=dif, op0=ALU.mult, op1=ALU.add))

        k_table = dram("k_table", (NP, D))
        v_table = dram("v_table", (NP, D))
        x3_table = dram("x3_table", (NP, D))
        y_table = dram("y_table", (YROWS, D))

        x_and_v = sb("x_and_v", [P, XT + NT, D])
        xall, v_all = x_and_v[:, 0:XT, :], x_and_v[:, XT:XT + NT, :]
        mv = sb("mv", [P, XT, 2])
        rstd = sb("rstd", [P, XT])
        bn_st = sb("bn_st", [P, XT, 6])
        mdif = sb("mdif", [P, XT])
        ident = sb("ident", [P, P])
        ones = sb("ones", [P, P])
        iota_b = sb("iota_b", [P, P], BF16)
        identb = sb("identb", [P, P], BF16)
        iota_row = sb("iota_row", [P, P])
        iota_i = sb("iota_i", [P, P], I32)
        part = sb("part", [P, EQ])
        partk = sb("partk", [P, 4])
        iota_s = sb("iota_s", [P, 8], I32)

        w_qkv = sb("w_qkv", [P, KC, 3 * D])
        b_qkv = sb("b_qkv", [P, 3 * D])
        qe = sb("qe", [P, KC])
        qe01 = sb("qe01", [P, KC])
        rel = sb("rel", [R, HD])
        rel02 = sb("rel02", [R, HD])

        w_o = sb("w_o", [P, KC, D])
        b_o = sb("b_o", [1, D])
        gamma = sb("gamma", [P, D])
        beta = sb("beta", [P, D])
        gate_w = sb("gate_w", [P, KC, NX])
        gate_b = sb("gate_b", [1, NX])
        nmr = sb("nmr", [P, XT])
        be_i = sb("be_i", [P, 2, BLOCKS], I32)
        xinc_i = sb("xinc_i", [P, NX], I32)
        slot_i = sb("slot_i", [P, BLOCKS], I32)
        pos_i = sb("pos_i", [P, NT, 2], I32)
        gates = sb("gates", [P, NT, 2])

        q_all = sb("q_all", [P, NT, D])
        src_idx = sb("src_idx", [P, STEPS], I32)
        dloc = sb("dloc", [P, STEPS + 2 * AHEAD])
        typ = sb("typ", [P, STEPS + 2 * AHEAD])
        dval = sb("dval", [P, STEPS])
        jk_i = sb("jk_i", [P, 2 + STEPS], I32)

        xn_st = sb("xn_st", [P, 2, D])
        enh_t = sb("enh_t", [P, 2, KC, P])
        k_all = sb("k_all", [P, NT, D + H])

        table_ctx = ExitStack()

        def tb(name, shape, dt=F32):
            return table_ctx.enter_context(nc.sbuf_tensor(name, shape, dt))

        tab_i = tb("tab_i", [EP, 3, EQ, P], I32)
        tab_f = tb("tab_f", [EP, 3, EQ, P])
        cnt = tb("cnt", [EP, NT])
        junk = tb("junk", [EP, EQ * P])
        rowm = tb("rowm", [P, 8, NT])
        rowi = tb("rowi", [P, 2, NT], I32)
        cmp3 = tb("cmp3", [SP_, 3, 4, NODE_TILES])
        stepc = tb("stepc", [SP_, 3, 4])
        diag = tb("diag", [SP_, 2, 4, SP_])
        rows = tb("rows", [P, 2, STEPS])
        sel = tb("sel", [EP, EQ, STEPS])
        tmp_s = tb("tmp_s", [P, 3, STEPS])
        table_ctx.close()

        edge_ctx = ExitStack()

        def eb(name, shape, dt=F32):
            return edge_ctx.enter_context(nc.sbuf_tensor(name, shape, dt))

        idx_st = eb("idx_st", [P, GRP // STG, STG], I32)
        ring = eb("ring", [P, GRP, D])
        hot = eb("hot", [P, 4, 2, P + R], BF16)
        hot_n = eb("hot_n", [P, 2, 2, P])
        hot_r = eb("hot_r", [R, 2, 2, P])
        dif = eb("dif", [P, 2, 2, P + R], BF16)
        prod = eb("prod", [P, 2 * D])
        score = eb("score", [P, STEPS * H])

        scratch = q_all[:, :, :].rearrange("p t c -> p (t c)")

        def carve(at, n):
            return scratch[0:SP_, at * 2048:at * 2048 + n]

        sc_t = carve(0, 2048).rearrange("p (q h e) -> p q h e", q=4, h=H)
        fwd = carve(1, 2048).rearrange("p (q h e) -> p q h e", q=4, h=H)
        bwd = carve(2, 2048).rearrange("p (q h e) -> p q h e", q=4, h=H)
        wgt = eb("wgt", [P, STEPS * H])

        acc = k_all
        hotf = eb("hotf", [P, 4, 2, P])
        wv = eb("wv", [P, 2, 2, D + H])

        dst_t = eb("dst_t", [SP_, 4, P])
        brk_f = eb("brk_f", [SP_, 4, P])
        brk_b = eb("brk_b", [SP_, 4, P])
        ends = eb("ends", [SP_, 4, 4, H])
        end_rows = eb("end_rows", [H, 4, STEPS])
        link = eb("link", [H, 2, STEPS + 1])
        hop = eb("hop", [H, 2, STEPS])
        run = eb("run", [H, 2, STEPS + 2])
        carry = eb("carry", [SP_, 4, 2, H])

        edge_ctx.close()

        msg = sb("msg", [P, 2, D])
        msg_t = sb("msg_t", [P, 2, D])
        xnb = sb("xnb", [P, 2, D])
        zero = sb("zero", [P, NT, H])
        rden = sb("rden", [P, NT, H])
        st = sb("st", [P, XT, 6])
        mv2 = sb("mv2", [P, XT, 2])
        rs2 = sb("rs2", [P, XT])
        logits = sb("logits", [P, NT, NX])
        top = sb("top", [P, NT, 8])
        top_i = sb("top_i", [P, NT, 8], U32)
        top_f = sb("top_f", [P, NT, 2])
        oh = sb("oh", [P, 2, NT, NX])
        cm = sb("cm", [P, NT, NX])
        pre = sb("pre", [P, NT, NX])
        tot = sb("tot", [P, NT, NX])
        cinc = sb("cinc", [P, NT, NX])
        xrow = sb("xrow", [P, 6, NX])
        xrow_i = sb("xrow_i", [P, NX], I32)
        tok = sb("tok", [P, NT])
        tok_i = sb("tok_i", [P, NT], I32)
        vmask = sb("vmask", [P, NT])
        pos = sb("pos", [P, NT, 2])
        hi_i = sb("hi_i", [P, NT, 2], I32)
        lo_i = sb("lo_i", [P, NT, 2], I32)
        hi_f = sb("hi_f", [P, NT, 2])
        lo_f = sb("lo_f", [P, NT, 2])
        lo_hot = q_all[:, :, :].rearrange("p t c -> p (t c)")[:, 0:NODE_TILES * 2 * P].rearrange("p (t k c) -> p t k c", t=NODE_TILES, k=2)
        hi_hot = sb("hi_hot", [P, NODE_TILES, 2, BLOCKS])
        beq = sb("beq", [P, BLOCKS, NX])
        bef = sb("bef", [P, BLOCKS])
        tri = sb("tri", [P, P])
        w_expert = x_and_v[:, :, :].rearrange("p t c -> p (t c)")[:, 0:WB * WX].rearrange("p (b n) -> p b n", b=WB)
        slot_st = sb("slot_st", [P, 2, 1], I32)
        xg = sb("xg", [P, 2, D])
        xg_t = sb("xg_t", [P, 2, D])
        act1 = sb("act1", [P, 2, HID])
        hid = sb("hid", [P, 2, HID])
        hid_t = sb("hid_t", [P, 2, HID])
        y_st = sb("y_st", [P, 2, D])
        pos_st = sb("pos_st", [P, CT, 2], I32)
        yab = q_all[:, :, :].rearrange("p (t k) c -> p t k c", k=2)[:, 0:CT, :, :]
        nmr2 = sb("nmr2", [P, NT])
        x3_all = v_all
        x2_all = acc

        bank = [ps(f"bank{i}", [P, 512]) for i in range(8)]

        s_x, s_edges, s_w, s_b, s_rel = (sem(n) for n in ("s_x", "s_edges", "s_w", "s_b", "s_rel"))
        s_pool, s_dve, s_pe, s_act = (sem(n) for n in ("s_pool", "s_dve", "s_pe", "s_act"))
        s_stat = Stage(sem("s_stat"))
        s_xn, s_xt, s_enh, s_qk, s_vv, s_qcp, s_kcp, s_vcp = (
            Stage(sem(n)) for n in ("s_xn", "s_xt", "s_enh", "s_qk", "s_vv", "s_qcp", "s_kcp", "s_vcp"))
        s_kst = [sem("s_kst0"), sem("s_kst1")]
        s_vst = [sem("s_vst0"), sem("s_vst1")]
        a_idx, a_dif, a_hot, a_tr, a_ev, a_mm, a_add, a_prod, a_red = (
            Stage(sem(n)) for n in ("a_idx", "a_dif", "a_hot", "a_tr", "a_ev", "a_mm", "a_add", "a_prod", "a_red"))
        got = [sem(f"got{i}") for i in range(GRP)]
        got_k, got_v, got_y = 0, 16 * TURNS, 2 * 16 * TURNS
        m_t, m_ends, m_back, m_w = (event(n) for n in ("m_t", "m_ends", "m_back", "m_w"))
        b_idx, b_dif, b_hot, b_wv, b_wc, b_mm, b_acc = (
            Stage(sem(n), 2 * GRP) for n in ("b_idx", "b_dif", "b_hot", "b_wv", "b_wc", "b_mm", "b_acc"))
        o_vz, o_xn, o_avg, o_msg, o_tr, o_ev, o_mm, o_sum, o_st, o_xb = (
            Stage(sem(n)) for n in ("o_vz", "o_xn", "o_avg", "o_msg", "o_tr", "o_ev", "o_mm", "o_sum", "o_st", "o_xb"))
        n_ga, n_x2, n_st = (Stage(sem(n)) for n in ("n_ga", "n_x2", "n_st"))
        g_tr, g_ev, g_mm, g_lg = (Stage(sem(n)) for n in ("g_tr", "g_ev", "g_mm", "g_lg"))
        r_lo, r_hi = sem("r_lo"), sem("r_hi")
        f_st, f_tx, f_xt, f_h, f_si, f_hid, f_th, f_ht, f_y, f_yc = (
            Stage(sem(n)) for n in ("f_st", "f_tx", "f_xt", "f_h", "f_si", "f_hid", "f_th", "f_ht", "f_y", "f_yc"))
        g_x3 = Stage(sem("g_x3"))
        s_wx, f_w = sem("s_wx"), Stage(sem("f_w"))
        s_xg = [sem(f"s_xg{i}") for i in range(2)]
        s_ys = [sem(f"s_ys{i}") for i in range(2)]
        c_st, c_a, c_o = (Stage(sem(n), CT) for n in ("c_st", "c_a", "c_o"))
        s_x3, s_w2, s_out = sem("s_x3"), sem("s_w2"), sem("s_out")
        s_pin = sem("s_pin")

        block = ctx.enter_context(nc.Block())

        @block.gpsimd
        def _(pool):
            c = Chain(pool, s_pool)
            c(pool.iota(iota_i[:, :], [[1, P]], base=0, channel_multiplier=0))
            c(pool.tensor_copy(iota_row[:, :], iota_i[:, :]))
            c(pool.iota(iota_s[:, 0:4], [[EP, 4]], base=0, channel_multiplier=1))
            c(pool.tensor_copy(part[:, :], iota_s[:, 0:4]))
            c(pool.iota(iota_s[:, 4:8], [[SP_, 4]], base=0, channel_multiplier=1))
            c(pool.tensor_copy(partk[:, :], iota_s[:, 4:8]))
            c(pool.memset(ones[:, :], 1.0))
            c(pool.memset(ident[:, :], 0.0))
            c(pool.affine_select(out=ident[:, :], in_=ident[:, :], compare_op=ALU.not_equal, fill=1.0, base=0,
                                 pattern=[[-1, P]], channel_multiplier=1))
            c(pool.tensor_copy(iota_b[:, :], iota_row[:, :]))
            c(pool.tensor_copy(identb[:, :], ident[:, :]))
            event("iota").set(pool)

            def gathers(table, staged, done):
                staged.open(pool)
                with pool.Fori(0, TURNS) as it:
                    for g in range(GRP // STG):
                        n = it * (GRP // STG) + g
                        done.hold(pool, n * (STG // 2) + (STG // 2 - 1) - PAIRS, s_pin)
                        pool.tensor_copy(idx_st[:, g, :], src_idx[:, bass.ds(it * GRP + g * STG, STG)]).then_inc(staged.sem, 1)
                        staged.hold(pool, n, s_pin)
                        for j in range(STG):
                            slot = g * STG + j
                            pool.indirect_dma_start(ring[:, slot, :], None, table, bass.IndirectOffsetOnAxis(ap=idx_st[:, g, j:j + 1], axis=0)).then_inc(got[slot], 16)

            event("tables").wait(pool)
            for b in range(2):
                pool.wait_ge(s_kst[b], 16 * (NT // 2))
            gathers(k_table, a_idx, a_prod)
            for b in range(2):
                pool.wait_ge(s_vst[b], 16 * (NT // 2))
            a_prod.wait(pool, TURNS * PAIRS - 1)
            gathers(v_table, b_idx, b_wv)

            o_vz.open(pool)
            o_xb.open(pool)
            event("zero").wait(pool)
            pool.wait_ge(s_w2, 96)
            with pool.Fori(0, NT) as t:
                a = tile_of(v_all, t).rearrange("p (h d) -> p h d", h=H)
                pool.tensor_tensor(a, a, tile_of(zero, t).unsqueeze(2).to_broadcast([P, H, HD]), ALU.mult).then_inc(o_vz.sem, 1)
            with pool.Fori(0, NT) as t:
                o_xn.hold(pool, t, s_pin)
                pool.tensor_tensor(tile_of(xall, t), tile_of(xall, t), beta[:, :], ALU.add).then_inc(o_xb.sem, 1)
            c(pool.iota(tok_i[:, :], [[P, NT]], base=0, channel_multiplier=1))
            c(pool.tensor_copy(tok[:, :], tok_i[:, :]))
            c(pool.affine_select(out=tri[:, :], in_=ones[:, :], compare_op=ALU.is_gt, fill=0.0, base=0,
                                 pattern=[[1, P]], channel_multiplier=-1))
            event("tri").set(pool)

            f_st.open(pool)
            event("slots").wait(pool)
            pool.wait_ge(s_x3, 16 * NT)

            def gather_x(b, i):
                f_tx.hold(pool, b - 2, s_pin)
                pool.tensor_copy(slot_st[:, i, :], slot_i[:, bass.ds(b, 1)]).then_inc(f_st.sem, 1)
                f_st.hold(pool, b, s_pin)
                pool.indirect_dma_start(xg[:, i, :], None, x3_table, bass.IndirectOffsetOnAxis(ap=slot_st[:, i, :], axis=0)).then_inc(s_xg[i], 16)

            with pool.Fori(0, BLOCKS // 2) as it:
                for i in range(2):
                    gather_x(it * 2 + i, i)
            c_st.open(pool)
            for i in range(2):
                pool.wait_ge(s_ys[i], 16 * (BLOCKS // 2))
            with pool.Fori(0, NT // CT) as it:
                c_o.hold(pool, it * CT - 1, s_pin)
                pool.tensor_copy(pos_st[:, :, :], pos_i[:, bass.ds(it * CT, CT), :]).then_inc(c_st.sem, 1)
                c_st.hold(pool, it, s_pin)
                for j in range(CT):
                    for k in range(2):
                        pool.indirect_dma_start(yab[:, j, k, :], None, y_table, bass.IndirectOffsetOnAxis(ap=pos_st[:, j, k:k + 1], axis=0)).then_inc(got[j], 16)

        @block.vector
        def _(v):
            c = Chain(v, s_dve)
            for s in (s_stat, s_xn, s_qcp, s_kcp, s_vcp):
                s.open(v)
            v.wait_ge(s_edges, 48)
            c(v.tensor_copy(tab_f[:, :, :, :], tab_i[:, :, :, :]))
            c(v.memset(cnt[:, 0:1], 0.0))
            dst_f = tab_f[:, 1, :, :].rearrange("p q c -> p (q c)")
            for j in range(1, NT):
                c(v.tensor_scalar(junk[:, :], dst_f, float(P * j), 0.0, ALU.is_lt, ALU.add, accum_out=cnt[:, j:j + 1]))
            event("cnt").set(v)
            v.wait_ge(s_pe, 1)
            s_j, n_j, lo, hi, c_j, inc, exc, a_j = (rowm[:, i, 0:NODE_TILES] for i in range(8))
            c(v.tensor_copy(rowm[:, 0, :], bank[0][:, 0:NT]))
            s_next = rowm[:, 0, 1:NT]
            c(v.tensor_tensor(n_j, s_next, s_j, ALU.subtract))
            c(v.tensor_copy(rowi[:, 0, 0:NODE_TILES], s_j))
            c(v.tensor_scalar(rowi[:, 1, 0:NODE_TILES], s_next, -1.0, None, ALU.add))
            c(v.tensor_scalar(rowi[:, :, 0:NODE_TILES], rowi[:, :, 0:NODE_TILES], 7, None, ALU.arith_shift_right))
            c(v.tensor_copy(lo, rowi[:, 0, 0:NODE_TILES]))
            c(v.tensor_copy(hi, rowi[:, 1, 0:NODE_TILES]))
            c(v.tensor_tensor(hi, hi, lo, ALU.subtract))
            c(v.tensor_scalar(n_j, n_j, 0.0, None, ALU.is_gt))
            c(v.scalar_tensor_tensor(out=c_j, in0=hi, scalar=1.0, in1=n_j, op0=ALU.add, op1=ALU.mult))
            c(v.memset(n_j, 1.0))
            c(v.tensor_tensor_scan(inc, n_j, c_j, 0.0, ALU.mult, ALU.add))
            c(v.tensor_tensor(exc, inc, c_j, ALU.subtract))
            c(v.tensor_tensor(a_j, lo, exc, ALU.subtract))
            event("iota").wait(v)
            v3 = [SP_, 4, NODE_TILES]
            kk = partk[0:SP_, :].unsqueeze(2).to_broadcast(v3)
            for i, bound in enumerate((inc, exc)):
                c(v.tensor_tensor(cmp3[:, i, :, :], bound[0:SP_, :].unsqueeze(1).to_broadcast(v3), kk, ALU.is_le))
            c(v.tensor_reduce(stepc[:, 1, :], cmp3[:, 0, :, :], AX.X, ALU.add))
            c(v.tensor_tensor(cmp3[:, 2, :, :], cmp3[:, 1, :, :], cmp3[:, 0, :, :], ALU.subtract))
            c(v.tensor_tensor(cmp3[:, 2, :, :], cmp3[:, 2, :, :], a_j[0:SP_, :].unsqueeze(1).to_broadcast(v3), ALU.mult))
            c(v.tensor_reduce(stepc[:, 2, :], cmp3[:, 2, :, :], AX.X, ALU.add))
            c(v.tensor_tensor(stepc[:, 0, :], stepc[:, 2, :], partk[0:SP_, :], ALU.add))
            for i in range(2):
                for q in range(4):
                    c(v.tensor_scalar(diag[:, i, q, :], ident[0:SP_, 0:SP_], stepc[:, i, q:q + 1], None, ALU.mult))
            event("diag").set(v)
            v.wait_ge(s_pe, 2)
            for i in range(2):
                c(v.tensor_copy(rows[:, i, :], bank[2 + i][:, 0:STEPS]))
            c(v.memset(jk_i[:, 0:2], 0.0))
            c(v.tensor_copy(jk_i[:, 2:2 + STEPS], rows[:, 1, :]))
            for q in range(EQ):
                c(v.tensor_scalar(sel[:, q, :], rows[0:EP, 0, :], part[0:EP, q:q + 1], None, ALU.is_equal))
            event("sel").set(v)
            v.wait_ge(s_pe, 3)
            c(v.tensor_copy(src_idx[:, :], bank[4][:, 0:STEPS]))
            c(v.memset(dloc[:, STEPS:STEPS + 2 * AHEAD], -1.0))
            c(v.memset(typ[:, STEPS:STEPS + 2 * AHEAD], -1.0))
            c(v.tensor_copy(typ[:, 0:STEPS], bank[6][:, 0:STEPS]))
            c(v.scalar_tensor_tensor(out=dloc[:, 0:STEPS], in0=rows[:, 1, :], scalar=-float(P), in1=bank[5][:, 0:STEPS], op0=ALU.mult, op1=ALU.add))
            c(v.tensor_scalar(tmp_s[:, 0, :], dloc[:, 0:STEPS], 0.0, None, ALU.is_ge))
            c(v.tensor_scalar(tmp_s[:, 1, :], dloc[:, 0:STEPS], float(P), None, ALU.is_lt))
            c(v.tensor_tensor(tmp_s[:, 0, :], tmp_s[:, 0, :], tmp_s[:, 1, :], ALU.mult))
            c(v.scalar_tensor_tensor(out=tmp_s[:, 2, :], in0=bank[5][:, 0:STEPS], scalar=1.0, in1=tmp_s[:, 0, :], op0=ALU.add, op1=ALU.mult))
            c(v.tensor_scalar(dval[:, :], tmp_s[:, 2, :], -1.0, None, ALU.add))
            event("tables").set(v)

            v.wait_ge(s_x, 16)
            with v.Fori(0, XT) as t:
                v.bn_stats(tile_of(bn_st, t), tile_of(xall, t)).then_inc(s_stat.sem, 1)
            s_stat.wait(v, XT - 1)
            row_stats(c, v, bn_st, mv, mdif[:, :])
            c(v.tensor_scalar(rstd[:, :], mv[:, :, 1], EPS, None, ALU.add))
            event("var").set(v)
            v.wait_ge(s_act, 3)
            c(v.reciprocal(rstd[:, :], rstd[:, :]))
            c(v.scalar_tensor_tensor(out=nmr[:, :], in0=mv[:, :, 0], scalar=-1.0, in1=rstd[:, :], op0=ALU.mult, op1=ALU.mult))
            v.wait_ge(s_b, 64)
            def norm(t, b):
                s_xt.wait(v, t - 2)
                v.tensor_scalar(xn_st[:, b, :], tile_of(xall, t),
                                mv[:, bass.ds(t, 1), 0], rstd[:, bass.ds(t, 1)], ALU.subtract, ALU.mult).then_inc(s_xn.sem, 1)
            norm(0, 0)
            with v.Fori(0, NT // 2) as it:
                for b in range(2):
                    t = it * 2 + b
                    norm(t + 1, 1 - b)
                    s_qk.wait(v, t)
                    v.tensor_tensor(tile_of(q_all, t), bank[2 + b][:, 0:D], b_qkv[:, 0:D], ALU.add).then_inc(s_qcp.sem, 1)
                    v.tensor_tensor(tile_of(k_all, t)[:, 0:D], bank[2 + b][:, D:2 * D], b_qkv[:, D:2 * D], ALU.add).then_inc(s_kcp.sem, 1)
                    s_vv.wait(v, t)
                    v.tensor_tensor(tile_of(v_all, t), bank[4 + b][:, 0:D], b_qkv[:, 2 * D:3 * D], ALU.add).then_inc(s_vcp.sem, 1)
            s_qcp.wait(v, NT - 1)

            for s in (a_add, a_prod, a_red):
                s.open(v)

            with v.Fori(0, TURNS) as it:
                for i in range(PAIRS):
                    n, b = it * PAIRS + i, i % 2
                    rows2 = ring[:, 2 * i:2 * i + 2, :]
                    ring4 = rows2.rearrange("p u (h d) -> p u h d", h=H)
                    for u in range(2):
                        v.wait_ge(got[2 * i + u], it * 16 + (got_k + 16))
                    a_mm.wait(v, n)
                    v.tensor_tensor(ring4, ring4, bank[4 + b][:, 0:2 * HD].rearrange("p (u d) -> p u d", u=2).unsqueeze(2).to_broadcast([P, 2, H, HD]), ALU.add).then_inc(a_add.sem, 1)
                    a_add.wait(v, n)
                    a_red.wait(v, n - 1)
                    v.tensor_tensor(prod[:, :], rows2.rearrange("p u c -> p (u c)"), bank[2 + b][:, :], ALU.mult).then_inc(a_prod.sem, 1)
                    a_prod.wait(v, n)
                    v.tensor_reduce(score[:, bass.ds(n * (2 * H), 2 * H)], prod[:, :].rearrange("p (g d) -> p g d", d=HD), AX.X, ALU.add).then_inc(a_red.sem, 1)
            a_red.wait(v, TURNS * PAIRS - 1)
            event("scores").set(v)

            m_t.wait(v)
            for q in range(4):
                c(v.tensor_copy(sc_t[:, q, :, :], bank[q][0:SP_, :].rearrange("p (h e) -> p h e", h=H)))
            c(v.tensor_copy(dst_t[:, :, :], bank[4][0:SP_, :].rearrange("p (q e) -> p q e", q=4)))
            c(v.memset(brk_f[:, :, 0:1], -BIG))
            c(v.memset(brk_b[:, :, P - 1:P], -BIG))
            c(v.tensor_tensor(brk_f[:, :, 1:P], dst_t[:, :, 1:P], dst_t[:, :, 0:P - 1], ALU.not_equal))
            c(v.tensor_scalar(brk_f[:, :, 1:P], brk_f[:, :, 1:P], -BIG, None, ALU.mult))
            c(v.tensor_copy(brk_b[:, :, 0:P - 1], brk_f[:, :, 1:P]))
            for q in range(4):
                for h in range(H):
                    v.tensor_tensor_scan(fwd[:, q, h, :], brk_f[:, q, :], sc_t[:, q, h, :], -BIG, ALU.add, ALU.max)
                    c(v.tensor_tensor_scan(bwd[:, q, h, ::-1], brk_b[:, q, ::-1], sc_t[:, q, h, ::-1], -BIG, ALU.add, ALU.max))
            c(v.tensor_copy(ends[:, :, 0, :], fwd[:, :, :, P - 1]))
            c(v.tensor_copy(ends[:, :, 1, :], bwd[:, :, :, 0]))
            c(v.tensor_copy(ends[:, :, 2, :], dst_t[:, :, 0:1].to_broadcast([SP_, 4, H])))
            c(v.tensor_copy(ends[:, :, 3, :], dst_t[:, :, P - 1:P].to_broadcast([SP_, 4, H])))
            event("ends").set(v)
            m_ends.wait(v)
            for i in range(4):
                c(v.tensor_copy(end_rows[:, i, :], bank[4 + i][0:H, 0:STEPS]))
            f_end, b_end, d_first, d_last = (end_rows[:, i, :] for i in range(4))
            c(v.memset(link[:, :, :], 0.0))
            c(v.tensor_tensor(link[:, 0, 1:STEPS], d_first[:, 1:STEPS], d_last[:, 0:STEPS - 1], ALU.is_equal))
            c(v.tensor_copy(link[:, 1, 0:STEPS - 1], link[:, 0, 1:STEPS]))
            c(v.tensor_tensor(hop[:, 0, :], d_first, d_last, ALU.is_equal))
            c(v.tensor_tensor(hop[:, 1, :], hop[:, 0, :], link[:, 1, 0:STEPS], ALU.mult))
            c(v.tensor_tensor(hop[:, 0, :], hop[:, 0, :], link[:, 0, 0:STEPS], ALU.mult))
            c(v.tensor_scalar(hop[:, :, :], hop[:, :, :], -1.0, BIG, ALU.add, ALU.mult))
            c(v.tensor_scalar(link[:, :, :], link[:, :, :], -1.0, BIG, ALU.add, ALU.mult))
            c(v.memset(run[:, :, :], -BIG))
            c(v.tensor_tensor_scan(run[:, 0, 1:STEPS + 1], hop[:, 0, :], f_end, -BIG, ALU.add, ALU.max))
            c(v.tensor_tensor_scan(run[:, 1, STEPS:0:-1], hop[:, 1, ::-1], b_end[:, ::-1], -BIG, ALU.add, ALU.max))
            c(v.tensor_tensor(hop[:, 0, :], run[:, 0, 0:STEPS], link[:, 0, 0:STEPS], ALU.add))
            c(v.tensor_tensor(hop[:, 1, :], run[:, 1, 2:STEPS + 2], link[:, 1, 0:STEPS], ALU.add))
            event("hop").set(v)
            m_back.wait(v)
            c(v.tensor_copy(carry[:, :, :, :], bank[4][0:SP_, 0:4 * 2 * H].rearrange("p (q i h) -> p q i h", q=4, i=2)))
            c(v.tensor_tensor(fwd, fwd, bwd, ALU.max))
            first = dst_t[:, :, 0:1].to_broadcast([SP_, 4, P])
            last = dst_t[:, :, P - 1:P].to_broadcast([SP_, 4, P])
            for i, (brk, edge) in enumerate(((brk_f, first), (brk_b, last))):
                c(v.tensor_tensor(brk[:, :, :], dst_t[:, :, :], edge, ALU.is_equal))
                c(v.tensor_scalar(brk[:, :, :], brk[:, :, :], -1.0, BIG, ALU.add, ALU.mult))
                for q in range(4):
                    for h in range(H):
                        ins = v.scalar_tensor_tensor(out=fwd[:, q, h, :], in0=brk[:, q, :], scalar=carry[:, q, i, h:h + 1],
                                                     in1=fwd[:, q, h, :], op0=ALU.add, op1=ALU.max)
                c(ins)
            c(v.tensor_tensor(sc_t, sc_t, fwd, ALU.subtract))
            event("diff").set(v)

            for s in (b_wv, b_acc):
                s.open(v)

            def weigh(it, i):
                n, b = it * PAIRS + i, i % 2
                for u in range(2):
                    v.wait_ge(got[2 * i + u], it * 16 + (got_v + 16))
                b_mm.wait(v, n - 2)
                v.tensor_tensor(wv[:, b, :, 0:D].rearrange("p u (h d) -> p u h d", h=H),
                                ring[:, 2 * i:2 * i + 2, :].rearrange("p u (h d) -> p u h d", h=H),
                                wgt[:, bass.ds(n * (2 * H), 2 * H)].rearrange("p (u h) -> p u h", u=2).unsqueeze(3).to_broadcast([P, 2, H, HD]),
                                ALU.mult).then_inc(b_wv.sem, 1)

            for b in range(2):
                v.wait_ge(s_kst[b], 16 * (NT // 2))
            c(v.memset(acc[:, :, :], 0.0))
            event("acc_0").set(v)
            m_w.wait(v)
            event("primed").wait(v)

            def add(n, b, u):
                tile = v.value_load(jk_i[0:1, bass.ds(n * 2 + u, 1)], min_val=0, max_val=NT - 1)
                b_mm.wait(v, n - 1)
                b_acc.wait(v, n * 2 + (u - 1))
                a = tile_of(acc, tile)
                v.tensor_tensor(a, a, bank[2 * b + u][:, 0:D + H], ALU.add).then_inc(b_acc.sem, 1)

            with v.Fori(0, TURNS) as it:
                for i in range(PAIRS):
                    weigh(it, i)
                    for u in range(2):
                        add(it * PAIRS + i, 1 - i % 2, u)
            for u in range(2):
                add(TURNS * PAIRS, 1, u)
            b_acc.wait(v, STEPS + 1)

            for s in (o_avg, o_msg, o_sum, o_st):
                s.open(v)
            c(v.tensor_scalar(zero[:, :, :], acc[:, :, D:D + H], 0.0, None, ALU.is_equal))
            event("zero").set(v)
            c(v.tensor_tensor(rden[:, :, :], acc[:, :, D:D + H], zero[:, :, :], ALU.add))
            c(v.reciprocal(rden[:, :, :], rden[:, :, :]))

            def average(t0):
                for b in range(2):
                    t = t0 + b
                    o_tr.wait(v, t - 2)
                    v.tensor_tensor(msg[:, b, :].rearrange("p (h d) -> p h d", h=H), tile_of(acc, t)[:, 0:D].rearrange("p (h d) -> p h d", h=H),
                                    tile_of(rden, t).unsqueeze(2).to_broadcast([P, H, HD]), ALU.mult).then_inc(o_avg.sem, 1)
                for b in range(2):
                    t = t0 + b
                    o_vz.wait(v, t)
                    o_avg.wait(v, t)
                    v.tensor_tensor(msg[:, b, :], msg[:, b, :], tile_of(v_all, t), ALU.add).then_inc(o_msg.sem, 1)

            def project(t0):
                for b in range(2):
                    t = t0 + b
                    o_mm.wait(v, t)
                    o_xn.wait(v, t)
                    v.tensor_tensor(tile_of(acc, t)[:, 0:D], bank[2 + b][:, 0:D], xnb[:, b, :], ALU.add).then_inc(o_sum.sem, 1)
                for b in range(2):
                    t = t0 + b
                    o_sum.wait(v, t)
                    v.bn_stats(tile_of(st, t), tile_of(acc, t)[:, 0:D]).then_inc(o_st.sem, 1)

            average(0)
            average(2)
            with v.Fori(0, NT // 2 - 2) as it:
                average(it * 2 + 4)
                project(it * 2)
            project(NT - 4)
            project(NT - 2)
            o_st.wait(v, NT - 1)

            def norm_stats(name, sqrt_n):
                row_stats(c, v, st[:, 0:NT, :], mv2[:, 0:NT, :], mdif[:, 0:NT])
                c(v.tensor_scalar(rs2[:, 0:NT], mv2[:, 0:NT, 1], EPS, None, ALU.add))
                event(name).set(v)
                v.wait_ge(s_act, sqrt_n)
                c(v.reciprocal(rs2[:, 0:NT], rs2[:, 0:NT]))

            norm_stats("var2", 9)
            for s in (n_ga, n_x2, n_st):
                s.open(v)
            with v.Fori(0, NT // 2) as it:
                for b in range(2):
                    t = it * 2 + b
                    a = tile_of(acc, t)[:, 0:D]
                    v.scalar_tensor_tensor(out=a, in0=a, scalar=mv2[:, bass.ds(t, 1), 0], in1=gamma[:, :], op0=ALU.subtract, op1=ALU.mult).then_inc(n_ga.sem, 1)
                for b in range(2):
                    t = it * 2 + b
                    a = tile_of(acc, t)[:, 0:D]
                    n_ga.wait(v, t)
                    o_xb.wait(v, t)
                    v.scalar_tensor_tensor(out=a, in0=a, scalar=rs2[:, bass.ds(t, 1)], in1=tile_of(xall, t), op0=ALU.mult, op1=ALU.add).then_inc(n_x2.sem, 1)
                for b in range(2):
                    t = it * 2 + b
                    n_x2.wait(v, t)
                    v.bn_stats(tile_of(st, t), tile_of(acc, t)[:, 0:D]).then_inc(n_st.sem, 1)
            n_st.wait(v, NT - 1)
            norm_stats("var3", 10)
            c(v.scalar_tensor_tensor(out=nmr2[:, :], in0=mv2[:, 0:NT, 0], scalar=-1.0, in1=rs2[:, 0:NT], op0=ALU.mult, op1=ALU.mult))
            event("nmr2").set(v)
            g_lg.open(v)

            def gate_rows(t0):
                for b in range(2):
                    t = t0 + b
                    g_tr.wait(v, t - 2)
                    v.tensor_scalar(msg[:, b, :], tile_of(x2_all, t)[:, 0:D], mv2[:, bass.ds(t, 1), 0], rs2[:, bass.ds(t, 1)], ALU.subtract, ALU.mult).then_inc(o_msg.sem, 1)

            def take_logits(t0):
                for b in range(2):
                    t = t0 + b
                    g_mm.wait(v, t)
                    v.tensor_scalar(tile_of(logits, t), bank[2 + b][:, 0:NX], 1.0, None, ALU.mult).then_inc(g_lg.sem, 1)

            gate_rows(0)
            gate_rows(2)
            with v.Fori(0, NT // 2 - 2) as it:
                gate_rows(it * 2 + 4)
                take_logits(it * 2)
            take_logits(NT - 4)
            take_logits(NT - 2)
            g_lg.wait(v, NT - 1)

            for t in range(NT):
                ins = v.max(top[:, t, :], logits[:, t, :])
            c(ins)
            for t in range(NT):
                ins = v.max_index(top_i[:, t, :], top[:, t, :], logits[:, t, :])
            c(ins)
            c(v.tensor_copy(top_f[:, :, :], top_i[:, :, 0:2]))
            c(v.tensor_tensor(gates[:, :, 1], top[:, :, 1], top[:, :, 0], ALU.subtract))
            event("dl").set(v)
            event("tri").wait(v)
            c(v.tensor_scalar(vmask[:, :], tok[:, :], float(N), None, ALU.is_lt))
            sh = [P, NT, NX]
            for k in range(2):
                c(v.tensor_tensor(oh[:, k, :, :], iota_row[:, 0:NX].unsqueeze(1).to_broadcast(sh), top_f[:, :, k:k + 1].to_broadcast(sh), ALU.is_equal))
                c(v.tensor_tensor(oh[:, k, :, :], oh[:, k, :, :], vmask[:, :].unsqueeze(2).to_broadcast(sh), ALU.mult))
            c(v.tensor_tensor(cm[:, :, :], oh[:, 0, :, :], oh[:, 1, :, :], ALU.add))
            event("cm").set(v)
            event("counts").wait(v)
            c(v.tensor_copy(pre[:, :, :], bank[0][:, 0:NT * NX].rearrange("p (t x) -> p t x", x=NX)))
            c(v.tensor_copy(tot[:, :, :], bank[1][:, 0:NT * NX].rearrange("p (t x) -> p t x", x=NX)))
            for x in range(NX):
                ins = v.tensor_tensor_scan(cinc[:, :, x], ones[:, 0:NT], tot[:, :, x], 0.0, ALU.mult, ALU.add)
            c(ins)
            x_cnt, x_nb, x_inc, x_base = (xrow[:, i, :] for i in range(4))
            c(v.tensor_scalar(x_cnt, cinc[:, NT - 1, :], float(P - 1), None, ALU.add))
            c(v.tensor_copy(xrow_i[:, :], x_cnt))
            c(v.tensor_scalar(xrow_i[:, :], xrow_i[:, :], 7, None, ALU.arith_shift_right))
            c(v.tensor_copy(x_nb, xrow_i[:, :]))
            c(v.tensor_tensor_scan(x_inc, ones[:, 0:NX], x_nb, 0.0, ALU.mult, ALU.add))
            c(v.tensor_tensor(x_base, x_inc, x_nb, ALU.subtract))
            c(v.tensor_scalar(x_base, x_base, float(P), None, ALU.mult))
            c(v.tensor_tensor(cinc[:, :, :], cinc[:, :, :], tot[:, :, :], ALU.subtract))
            c(v.tensor_tensor(cinc[:, :, :], cinc[:, :, :], pre[:, :, :], ALU.add))
            c(v.tensor_tensor(cinc[:, :, :], cinc[:, :, :], x_base.unsqueeze(1).to_broadcast(sh), ALU.add))
            for k in range(2):
                c(v.tensor_tensor(oh[:, k, :, :], oh[:, k, :, :], cinc[:, :, :], ALU.mult))
                c(v.tensor_reduce(pos[:, :, k], oh[:, k, :, :], AX.X, ALU.add))
            sb_ = [P, BLOCKS, NX]
            c(v.tensor_tensor(beq[:, :, :], x_inc.unsqueeze(1).to_broadcast(sb_), iota_row[:, 0:BLOCKS].unsqueeze(2).to_broadcast(sb_), ALU.is_le))
            c(v.tensor_reduce(bef[:, :], beq[:, :, :], AX.X, ALU.add))
            c(v.tensor_scalar(be_i[:, 0, :], bef[:, :], float(NX - 1), None, ALU.min))
            c(v.tensor_scalar(be_i[:, 1, :], be_i[:, 0, :], WB - 1, None, ALU.bitwise_and))
            c(v.tensor_copy(xinc_i[:, :], x_inc))
            event("blocks").set(v)
            c(v.tensor_copy(pos_i[:, :, :], pos[:, :, :]))
            c(v.tensor_scalar(hi_i[:, :, :], pos_i[:, :, :], 7, None, ALU.arith_shift_right))
            c(v.tensor_scalar(lo_i[:, :, :], pos_i[:, :, :], P - 1, None, ALU.bitwise_and))
            c(v.tensor_copy(hi_f[:, :, :], hi_i[:, :, :]))
            c(v.tensor_copy(lo_f[:, :, :], lo_i[:, :, :]))
            c(v.tensor_scalar(vmask[:, :], vmask[:, :], -1.0, -float(4 * BLOCKS), ALU.add, ALU.mult))
            c(v.tensor_tensor(hi_f[:, :, :], hi_f[:, :, :], vmask[:, :].unsqueeze(2).to_broadcast([P, NT, 2]), ALU.add))
            for a in range(0, NODE_TILES, SLOT_TILES):
                n = [P, SLOT_TILES, 2, P]
                m = [P, SLOT_TILES, 2, BLOCKS]
                w = slice(a, a + SLOT_TILES)
                v.tensor_tensor(lo_hot[:, w, :, :], iota_row[:, :].unsqueeze(1).unsqueeze(1).to_broadcast(n), lo_f[:, w, :].unsqueeze(3).to_broadcast(n), ALU.is_equal).then_inc(r_lo, 1)
                c(v.tensor_tensor(hi_hot[:, w, :, :], iota_row[:, 0:BLOCKS].unsqueeze(1).unsqueeze(1).to_broadcast(m), hi_f[:, w, :].unsqueeze(3).to_broadcast(m), ALU.is_equal))
                v.tensor_tensor(hi_hot[:, w, :, :], hi_hot[:, w, :, :], tok[:, w].unsqueeze(2).unsqueeze(3).to_broadcast(m), ALU.mult).then_inc(r_hi, 1)
            event("slot_sum").wait(v)
            c(v.tensor_copy(slot_i[:, :], bank[4][:, 0:BLOCKS]))
            event("slots").set(v)
            event("dexp").wait(v)
            c(v.tensor_scalar(gates[:, :, 0], gates[:, :, 1], 1.0, None, ALU.add))
            c(v.reciprocal(gates[:, :, 0], gates[:, :, 0]))
            c(v.tensor_tensor(gates[:, :, 1], gates[:, :, 1], gates[:, :, 0], ALU.mult))

            for s in (f_hid, f_yc):
                s.open(v)

            def gated(b, i):
                f_si.wait(v, b)
                f_th.wait(v, b - 2)
                v.tensor_tensor(hid[:, i, :], act1[:, i, :], bank[3 + i][:, :], ALU.mult).then_inc(f_hid.sem, 1)

            def take_y(b, i, first):
                f_y.wait(v, b)
                if not first:
                    v.wait_ge(s_ys[i], ys_done(b))
                v.tensor_copy(y_st[:, i, :], bank[6 + i][:, 0:D]).then_inc(f_yc.sem, 1)

            def ys_done(b):
                return (b // 2) * 16

            gated(0, 0)
            gated(1, 1)
            take_y(0, 0, True)
            gated(2, 0)
            take_y(1, 1, True)
            with v.Fori(0, (BLOCKS - 4) // 2) as it:
                for i in range(2):
                    gated(it * 2 + 3 + i, 1 - i)
                    f_y.wait(v, it * 2 + 2 + i)
                    v.wait_ge(s_ys[i], it * 16 + 16)
                    v.tensor_copy(y_st[:, i, :], bank[6 + i][:, 0:D]).then_inc(f_yc.sem, 1)
            gated(BLOCKS - 1, 1)
            for b in (BLOCKS - 2, BLOCKS - 1):
                take_y(b, b % 2, False)
            for s in (c_a, c_o):
                s.open(v)
            with v.Fori(0, NT // CT) as it:
                for j in range(CT):
                    t = it * CT + j
                    a = tile_of(x2_all, t)[:, 0:D]
                    v.wait_ge(got[j], it * 32 + (got_y + 32))
                    for k in range(2):
                        if k:
                            c_a.wait(v, t)
                        v.scalar_tensor_tensor(out=a, in0=yab[:, j, k, :], scalar=tile_of(gates, t)[:, k:k + 1], in1=a,
                                               op0=ALU.mult, op1=ALU.add).then_inc((c_o if k else c_a).sem, 1)

        @block.sync
        def _(sp):
            for i, name in enumerate(("src", "dst", "typ")):
                sp.dma_start(tab_i[:, i, :, :], A[name].rearrange("(q p c) -> p q c", p=EP, c=P)).then_inc(s_edges, 16)
            sp.dma_start(xall[:, :, :], A["x"].rearrange("(t p) c -> p t c", p=P)).then_inc(s_x, 16)
            sp.dma_start(rel[:, :], A["rel_w"]).then_inc(s_rel, 16)
            with sp.Fori(0, NT // 2) as it:
                for b in range(2):
                    t = sp.snap(it * 2 + b)
                    row = sp.snap(t * P)
                    s_kcp.hold(sp, t, s_pin)
                    sp.dma_start(k_table[bass.ds(row, P), :], tile_of(k_all, t)[:, 0:D]).then_inc(s_kst[b], 16)
                    s_vcp.hold(sp, t, s_pin)
                    sp.dma_start(v_table[bass.ds(row, P), :], tile_of(v_all, t)).then_inc(s_vst[b], 16)
            with sp.Fori(0, NT) as t:
                row = sp.snap(t * P)
                g_x3.hold(sp, t, s_pin)
                sp.dma_start(x3_table[bass.ds(row, P), :], tile_of(x3_all, t)).then_inc(s_x3, 16)
            event("blocks").wait(sp)
            f_w.open(sp)

            def load_expert(e, i, done):
                for k, name in enumerate(("w1", "w2")):
                    sp.dma_start(w_expert[:, i, k * KC * HID:(k + 1) * KC * HID].rearrange("p (c n) -> p c n", c=KC),
                                 A[name][bass.ds(e, 1), :, :].rearrange("e (c p) n -> p (e c) n", p=P)).then_inc(s_wx, 16)
                sp.dma_start(w_expert[:, i, 2 * KC * HID:WX].rearrange("p (c n) -> p c n", c=HC),
                             A["w3"][bass.ds(e, 1), :, :].rearrange("e (c p) n -> p (e c) n", p=P)).then_inc(s_wx, 16)
                sp.wait_ge(s_wx, done)
                sp.sem_inc(f_w.sem, 1)

            for e in range(WB):
                if e == 2:
                    sp.wait_ge(s_x3, 16 * NT)
                load_expert(e, e, 48 * (e + 1))
            with sp.Fori(0, NX // WB - 1) as it:
                for i in range(WB):
                    e = sp.snap(it * WB + (WB + i))
                    last = sp.value_load(xinc_i[0:1, bass.ds(it * WB + i, 1)], min_val=0, max_val=BLOCKS)
                    f_y.hold(sp, last - 1, s_pin)
                    load_expert(e, i, it * (48 * WB) + 48 * (WB + 1 + i))
            with sp.Fori(0, NT) as t:
                row = sp.snap(t * P)
                c_o.hold(sp, t, s_pin)
                sp.dma_start(out[bass.ds(row, P), :], tile_of(x2_all, t)[:, 0:D]).then_inc(s_out, 16)
            sp.wait_ge(s_out, 16 * NT)

        @block.scalar
        def _(act):
            for i, n in enumerate(("Wq", "Wk", "Wv")):
                act.dma_start(w_qkv[:, :, i * D:(i + 1) * D], A[n].rearrange("(c p) n -> p c n", p=P)).then_inc(s_w, 16)
            for i, n in enumerate(("bq", "bk", "bv")):
                act.dma_start(b_qkv[:, i * D:(i + 1) * D], bcast(A[n])).then_inc(s_b, 16)
            act.dma_start(qe[:, :], A["query_emb"].rearrange("(c p) -> p c", p=P), allow_slow_non_contiguous=True).then_inc(s_b, 16)
            act.dma_start(w_o[:, :, :], A["Wo"].rearrange("(c p) n -> p c n", p=P)).then_inc(s_w2, 16)
            act.dma_start(gate_w[:, :, :], A["gate_w"].rearrange("(c p) n -> p c n", p=P)).then_inc(s_w2, 16)
            act.dma_start(gamma[:, :], bcast(A["gamma"])).then_inc(s_w2, 16)
            act.dma_start(beta[:, :], bcast(A["beta"])).then_inc(s_w2, 16)
            act.dma_start(b_o[:, :], A["bo"].rearrange("(a n) -> a n", a=1)).then_inc(s_w2, 16)
            act.dma_start(gate_b[:, :], A["gate_b"].rearrange("(a n) -> a n", a=1)).then_inc(s_w2, 16)
            act.wait_ge(s_b, 64)
            act.wait_ge(s_rel, 16)
            act.activation(qe01[:, :], qe[:, :], ACT.Copy, scale=0.1).then_inc(s_act, 1)
            act.activation(rel02[:, :], rel[:, :], ACT.Copy, scale=0.2).then_inc(s_act, 1)
            event("var").wait(act)
            act.activation(rstd[:, :], rstd[:, :], ACT.Sqrt).then_inc(s_act, 1)
            act.wait_ge(s_act, 2)
            s_enh.open(act)
            with act.Fori(0, NT // 2) as it:
                for b in range(2):
                    t = it * 2 + b
                    s_qk.wait(act, t - 2)
                    s_xt.wait(act, t)
                    for c in range(KC):
                        ins = act.activation(enh_t[:, b, c, :], bank[b][:, c * P:(c + 1) * P], ACT.Identity,
                                             bias=qe01[:, c:c + 1])
                    ins.then_inc(s_enh.sem, 1)

            for s in (a_dif, a_hot, a_ev):
                s.open(act)

            def hot_dif(n, b):
                for u in range(2):
                    act.activation(dif[:, b, u, 0:P], iota_b[:, :], ACT.Abs, bias=dloc[:, bass.ds(n * 2 + u, 1)], scale=-1.0)
                    ins = act.activation(dif[:, b, u, P:P + R], iota_b[:, 0:R], ACT.Abs, bias=typ[:, bass.ds(n * 2 + u, 1)], scale=-1.0)
                ins.then_inc(a_dif.sem, 1)

            def hot_relu(n, b, hb):
                a_dif.wait(act, n)
                a_tr.wait(act, n - 4)
                act.activation(hot[:, hb, :, :], dif[:, b, :, :], ACT.Relu, bias=ones[:, 0:1], scale=-1.0).then_inc(a_hot.sem, 1)

            event("tables").wait(act)
            for n in range(AHEAD):
                hot_dif(n, n % 2)
                hot_relu(n, n % 2, n)
            with act.Fori(0, TURNS) as it:
                for i in range(PAIRS):
                    n, b = it * PAIRS + i, i % 2
                    hot_dif(n + AHEAD, (i + AHEAD) % 2)
                    a_mm.wait(act, n - 2)
                    a_tr.wait(act, n)
                    t = bank[b][:, :].bitcast(BF16)[:, 0:4 * P].rearrange("p (u x) -> p u x", u=2)
                    act.activation(hot_n[:, b, :, :], t[:, :, 0:P], ACT.Copy)
                    act.activation(hot_r[:, b, :, :], t[0:R, :, P:2 * P], ACT.Copy).then_inc(a_ev.sem, 1)
                    hot_relu(n + AHEAD, (i + AHEAD) % 2, (i + AHEAD) % 4)
            event("diff").wait(act)
            act.activation(sc_t, sc_t, ACT.Exp, scale=HD ** -0.5).then_inc(s_act, 1)
            act.wait_ge(s_act, 4)
            event("exp").set(act)
            event("w_t").wait(act)
            wgt4 = wgt[:, :].rearrange("p (q k h) -> p q h k", q=4, h=H)
            for q in range(4):
                act.activation(wgt4[:, q, :, :], bank[q][:, 0:H * SP_].rearrange("p (h k) -> p h k", h=H), ACT.Copy).then_inc(s_act, 1)
            act.wait_ge(s_act, 8)
            m_w.set(act)
            for s in (b_dif, b_hot, b_wc):
                s.open(act)

            def hotf_dif(n, b):
                for u in range(2):
                    ins = act.activation(dif[:, b, u, 0:P], iota_b[:, :], ACT.Abs, bias=dloc[:, bass.ds(n * 2 + u, 1)], scale=-1.0)
                ins.then_inc(b_dif.sem, 1)

            def hotf_relu(n, b, hb):
                b_dif.wait(act, n)
                b_mm.wait(act, n - 4)
                act.activation(hotf[:, hb, :, :], dif[:, b, :, 0:P], ACT.Relu, bias=ones[:, 0:1], scale=-1.0).then_inc(b_hot.sem, 1)

            for n in range(AHEAD):
                hotf_dif(n, n % 2)
                hotf_relu(n, n % 2, n)
            with act.Fori(0, TURNS) as it:
                for i in range(PAIRS):
                    n, b = it * PAIRS + i, i % 2
                    hotf_dif(n + AHEAD, (i + AHEAD) % 2)
                    b_mm.wait(act, n - 2)
                    act.activation(wv[:, b, :, D:D + H], wgt[:, bass.ds(n * (2 * H), 2 * H)].rearrange("p (u h) -> p u h", u=2), ACT.Copy).then_inc(b_wc.sem, 1)
                    hotf_relu(n + AHEAD, (i + AHEAD) % 2, (i + AHEAD) % 4)
            o_xn.open(act)
            o_ev.open(act)
            act.wait_ge(s_w2, 96)

            def normalize(t0):
                for b in range(2):
                    t = t0 + b
                    o_sum.wait(act, t - 2)
                    act.activation(xnb[:, b, :], tile_of(xall, t), ACT.Identity, bias=nmr[:, bass.ds(t, 1)], scale=rstd[:, bass.ds(t, 1)]).then_inc(o_xn.sem, 1)

            def take_transposes(t0, tr, mm, ev):
                for b in range(2):
                    t = t0 + b
                    tr.wait(act, t)
                    mm.wait(act, t - 2)
                    act.activation(msg_t[:, b, :], bank[b][:, 0:D], ACT.Copy).then_inc(ev.sem, 1)

            normalize(0)
            take_transposes(0, o_tr, o_mm, o_ev)
            with act.Fori(0, NT // 2 - 1) as it:
                take_transposes(it * 2 + 2, o_tr, o_mm, o_ev)
                normalize(it * 2 + 2)
            for i, name in enumerate(("var2", "var3")):
                event(name).wait(act)
                act.activation(rs2[:, 0:NT], rs2[:, 0:NT], ACT.Sqrt).then_inc(s_act, 1)
            g_ev.open(act)
            g_x3.open(act)
            event("nmr2").wait(act)

            def expert_rows(t0):
                for b in range(2):
                    t = t0 + b
                    act.activation(tile_of(x3_all, t), tile_of(x2_all, t)[:, 0:D], ACT.Identity, bias=nmr2[:, bass.ds(t, 1)], scale=rs2[:, bass.ds(t, 1)]).then_inc(g_x3.sem, 1)

            take_transposes(0, g_tr, g_mm, g_ev)
            with act.Fori(0, NT // 2 - 1) as it:
                expert_rows(it * 2)
                take_transposes(it * 2 + 2, g_tr, g_mm, g_ev)
            expert_rows(NT - 2)
            event("dl").wait(act)
            act.activation(gates[:, :, 1], gates[:, :, 1], ACT.Exp).then_inc(s_act, 1)
            act.wait_ge(s_act, 11)
            event("dexp").set(act)
            for s in (f_xt, f_si, f_ht):
                s.open(act)

            def copy_xt(b, i):
                f_tx.wait(act, b)
                f_h.wait(act, b - 2)
                act.activation(xg_t[:, i, :], bank[0][:, 0:D], ACT.Copy).then_inc(f_xt.sem, 1)

            def silu(b, i):
                f_h.wait(act, b)
                f_hid.wait(act, b - 2)
                act.activation(act1[:, i, :], bank[1 + i][:, :], ACT.Silu).then_inc(f_si.sem, 1)

            def copy_ht(b, i):
                f_th.wait(act, b)
                f_y.wait(act, b - 2)
                act.activation(hid_t[:, i, :], bank[5][:, :], ACT.Copy).then_inc(f_ht.sem, 1)

            def store_y(b, i):
                row = act.snap(b * P)
                f_yc.hold(act, b, s_pin)
                act.dma_start(y_table[bass.ds(row, P), :], y_st[:, i, :]).then_inc(s_ys[i], 16)

            copy_xt(0, 0)
            silu(0, 0)
            copy_xt(1, 1)
            copy_ht(0, 0)
            silu(1, 1)
            copy_xt(2, 0)
            copy_ht(1, 1)
            store_y(0, 0)
            silu(2, 0)
            copy_xt(3, 1)
            with act.Fori(0, BLOCKS // 2 - 2) as it:
                for i in range(2):
                    b = it * 2 + 3 + i
                    copy_ht(b - 1, i)
                    store_y(b - 2, 1 - i)
                    silu(b, 1 - i)
                    copy_xt(b + 1, i)
            copy_ht(BLOCKS - 2, 0)
            store_y(BLOCKS - 3, 1)
            silu(BLOCKS - 1, 1)
            copy_ht(BLOCKS - 1, 1)
            for i in range(2):
                store_y(BLOCKS - 2 + i, i)

        @block.tensor
        def _(pe):
            s_xt.open(pe)
            s_qk.open(pe)
            s_vv.open(pe)
            event("iota").wait(pe)
            event("cnt").wait(pe)
            pe.matmul(bank[0][:, 0:NT], ones[0:EP, :], cnt[:, :], start=True, stop=True).then_inc(s_pe, 1)
            event("diag").wait(pe)
            for v in range(2):
                for q in range(4):
                    ins = pe.matmul(bank[2 + v][:, q * SP_:(q + 1) * SP_], ones[0:SP_, :], diag[:, v, q, :],
                                    start=True, stop=True)
            ins.then_inc(s_pe, 1)
            event("sel").wait(pe)
            for i in range(3):
                for q in range(EQ):
                    ins = pe.matmul(bank[4 + i][:, 0:STEPS], tab_f[:, i, q, :], sel[:, q, :], start=(q == 0), stop=(q == EQ - 1))
            ins.then_inc(s_pe, 1)
            pe.wait_ge(s_w, 48)
            def transposes(t, b):
                s_xn.wait(pe, t)
                s_enh.wait(pe, t - 2)
                for c in range(KC):
                    ins = pe.transpose(bank[b][:, c * P:(c + 1) * P], xn_st[:, b, c * P:(c + 1) * P], ident[:, :])
                ins.then_inc(s_xt.sem, 1)
            with pe.Fori(0, NT // 2) as it:
                for b in range(2):
                    t = it * 2 + b
                    transposes(t, b)
                    s_enh.wait(pe, t)
                    s_kcp.wait(pe, t - 2)
                    for c in range(KC):
                        ins = pe.matmul(bank[2 + b][:, :], enh_t[:, b, c, :], w_qkv[:, c, 0:2 * D], start=(c == 0), stop=(c == KC - 1))
                    ins.then_inc(s_qk.sem, 1)
                    s_vcp.wait(pe, t - 2)
                    for c in range(KC):
                        ins = pe.matmul(bank[4 + b][:, 0:D], enh_t[:, b, c, :], w_qkv[:, c, 2 * D:3 * D], start=(c == 0), stop=(c == KC - 1))
                    ins.then_inc(s_vv.sem, 1)

            a_tr.open(pe)
            a_mm.open(pe)

            def hot_transposes(n, b, hb):
                a_hot.wait(pe, n)
                a_ev.wait(pe, n - 2)
                t = bank[b][:, :].bitcast(BF16)
                for u in range(2):
                    pe.transpose(t[:, 2 * u * P:(2 * u + 1) * P], hot[:, hb, u, 0:P], identb[:, :])
                    ins = pe.transpose(t[0:R, (2 * u + 1) * P:(2 * u + 2) * P], hot[:, hb, u, P:P + R], identb[:, :])
                ins.then_inc(a_tr.sem, 1)

            s_vcp.wait(pe, NT - 1)
            hot_transposes(0, 0, 0)
            with pe.Fori(0, TURNS) as it:
                for i in range(PAIRS):
                    n, b = it * PAIRS + i, i % 2
                    tiles = [pe.value_load(jk_i[0:1, bass.ds(n * 2 + u + 2, 1)], min_val=0, max_val=NT - 1) for u in range(2)]
                    hot_transposes(n + 1, 1 - b, (i + 1) % 4)
                    a_ev.wait(pe, n)
                    a_prod.wait(pe, n - 2)
                    for u in range(2):
                        pe.matmul(bank[2 + b][:, u * D:(u + 1) * D], hot_n[:, b, u, :], tile_of(q_all, tiles[u]), start=True, stop=True)
                        ins = pe.matmul(bank[4 + b][:, u * HD:(u + 1) * HD], hot_r[:, b, u, :], rel02[:, :], start=True, stop=True)
                    ins.then_inc(a_mm.sem, 1)

            def done(ins, what):
                pe_n[0] += 1
                ins.then_inc(s_pe, 1)
                pe.wait_ge(s_pe, pe_n[0])
                what.set(pe)

            pe_n = [3]
            event("scores").wait(pe)
            score4 = score[:, :].rearrange("p (q k h) -> p q h k", q=4, h=H)
            for q in range(4):
                for h in range(H):
                    pe.transpose(bank[q][0:SP_, h * P:(h + 1) * P], score4[:, q, h, :], ident[:, :])
                ins = pe.transpose(bank[4][0:SP_, q * P:(q + 1) * P], dval[:, q * SP_:(q + 1) * SP_], ident[:, :])
            done(ins, m_t)
            event("ends").wait(pe)
            for i in range(4):
                for q in range(4):
                    ins = pe.transpose(bank[4 + i][0:H, q * SP_:(q + 1) * SP_], ends[:, q, i, :], ident[0:SP_, 0:SP_])
            done(ins, m_ends)
            event("hop").wait(pe)
            for q in range(4):
                for i in range(2):
                    ins = pe.transpose(bank[4][0:SP_, (q * 2 + i) * H:(q * 2 + i + 1) * H], hop[:, i, q * SP_:(q + 1) * SP_], ident[0:H, 0:H])
            done(ins, m_back)
            event("exp").wait(pe)
            for q in range(4):
                for h in range(H):
                    ins = pe.transpose(bank[q][:, h * SP_:(h + 1) * SP_], sc_t[:, q, h, :], ident[0:SP_, 0:SP_])
            done(ins, event("w_t"))

            b_mm.open(pe)
            m_w.wait(pe)
            event("acc_0").wait(pe)
            for u in range(2):
                ins = pe.matmul(bank[2 + u][:, 0:D + H], acc[:, 0, 0:P], acc[:, 1, :], start=True, stop=True)
            done(ins, event("primed"))
            with pe.Fori(0, TURNS) as it:
                for i in range(PAIRS):
                    n, b = it * PAIRS + i, i % 2
                    b_hot.wait(pe, n)
                    b_wv.wait(pe, n)
                    b_wc.wait(pe, n)
                    b_acc.wait(pe, n * 2 - 1)
                    for u in range(2):
                        ins = pe.matmul(bank[2 * b + u][:, 0:D + H], hotf[:, i % 4, u, :], wv[:, b, u, :], start=True, stop=True)
                    ins.then_inc(b_mm.sem, 1)

            o_tr.open(pe)
            o_mm.open(pe)
            pe.wait_ge(s_w2, 96)
            b_acc.wait(pe, STEPS + 1)

            def turn_rows(t0, msg_at, tr, ev):
                for b in range(2):
                    t = t0 + b
                    o_msg.wait(pe, t + msg_at)
                    ev.wait(pe, t - 2)
                    for c in range(KC):
                        ins = pe.transpose(bank[b][:, c * P:(c + 1) * P], msg[:, b, c * P:(c + 1) * P], ident[:, :])
                    ins.then_inc(tr.sem, 1)

            def times(t0, w, bias, ev, mm, taken):
                n = w.shape[2]
                for b in range(2):
                    t = t0 + b
                    ev.wait(pe, t)
                    taken.wait(pe, t - 2)
                    for c in range(KC):
                        pe.matmul(bank[2 + b][:, 0:n], msg_t[:, b, c * P:(c + 1) * P], w[:, c, :], start=(c == 0), stop=False)
                    pe.matmul(bank[2 + b][:, 0:n], ones[0:1, :], bias[:, :], start=False, stop=True).then_inc(mm.sem, 1)

            turn_rows(0, 0, o_tr, o_ev)
            with pe.Fori(0, NT // 2 - 1) as it:
                turn_rows(it * 2 + 2, 0, o_tr, o_ev)
                times(it * 2, w_o, b_o, o_ev, o_mm, o_sum)
            times(NT - 2, w_o, b_o, o_ev, o_mm, o_sum)
            g_tr.open(pe)
            g_mm.open(pe)
            turn_rows(0, NT, g_tr, g_ev)
            with pe.Fori(0, NT // 2 - 1) as it:
                turn_rows(it * 2 + 2, NT, g_tr, g_ev)
                times(it * 2, gate_w, gate_b, g_ev, g_mm, g_lg)
            times(NT - 2, gate_w, gate_b, g_ev, g_mm, g_lg)
            event("cm").wait(pe)
            cmf = cm[:, :, :].rearrange("p t x -> p (t x)")
            pe.matmul(bank[0][:, 0:NT * NX], tri[:, :], cmf, start=True, stop=True)
            done(pe.matmul(bank[1][:, 0:NT * NX], ones[:, :], cmf, start=True, stop=True), event("counts"))
            slots = bank[4][:, 0:BLOCKS]
            for t in range(NODE_TILES):
                if t % SLOT_TILES == 0:
                    pe.wait_ge(r_lo, t // SLOT_TILES + 1)
                    pe.wait_ge(r_hi, t // SLOT_TILES + 1)
                for k in range(2):
                    ins = pe.matmul(slots, lo_hot[:, t, k, :], hi_hot[:, t, k, :], start=(t + k == 0), stop=(t + k == NODE_TILES))
            done(ins, event("slot_sum"))

            for s in (f_tx, f_h, f_th, f_y):
                s.open(pe)
            event("slots").wait(pe)

            def turn_x(b, i, got):
                pe.wait_ge(s_xg[i], got)
                f_xt.wait(pe, b - 1)
                for c in range(KC):
                    ins = pe.transpose(bank[0][:, c * P:(c + 1) * P], xg[:, i, c * P:(c + 1) * P], ident[:, :])
                ins.then_inc(f_tx.sem, 1)

            def weights_of(b):
                e, buf = (pe.value_load(be_i[0:1, k, bass.ds(b, 1)], min_val=0, max_val=top) for k, top in enumerate((NX - 1, WB - 1)))
                return e, w_expert[:, bass.ds(buf, 1), :].rearrange("p a n -> p (a n)")

            def first_half(b, i, e, w):
                f_xt.wait(pe, b)
                f_hid.wait(pe, b - 2)
                f_w.wait(pe, e)
                for m in range(2):
                    for c in range(KC):
                        at = (m * KC + c) * HID
                        ins = pe.matmul(bank[1 + 2 * m + i][:, :], xg_t[:, i, c * P:(c + 1) * P], w[:, at:at + HID], start=(c == 0), stop=(c == KC - 1))
                ins.then_inc(f_h.sem, 1)

            def turn_hid(b, i):
                f_hid.wait(pe, b)
                f_ht.wait(pe, b - 1)
                for c in range(HC):
                    ins = pe.transpose(bank[5][:, c * P:(c + 1) * P], hid[:, i, c * P:(c + 1) * P], ident[:, :])
                ins.then_inc(f_th.sem, 1)

            def second_half(b, i, w):
                f_ht.wait(pe, b)
                f_yc.wait(pe, b - 2)
                for c in range(HC):
                    at = 2 * KC * HID + c * D
                    ins = pe.matmul(bank[6 + i][:, 0:D], hid_t[:, i, c * P:(c + 1) * P], w[:, at:at + D], start=(c == 0), stop=(c == HC - 1))
                ins.then_inc(f_y.sem, 1)

            turn_x(0, 0, 16)
            first_half(0, 0, *weights_of(0))
            turn_x(1, 1, 16)
            with pe.Fori(0, BLOCKS // 2 - 1) as it:
                for i in range(2):
                    b = it * 2 + 1 + i
                    w_before, (e, w) = weights_of(b - 1)[1], weights_of(b)
                    turn_hid(b - 1, i)
                    first_half(b, 1 - i, e, w)
                    turn_x(b + 1, i, it * 16 + 32)
                    second_half(b - 1, i, w_before)
            w_before, (e, w) = weights_of(BLOCKS - 2)[1], weights_of(BLOCKS - 1)
            turn_hid(BLOCKS - 2, 0)
            first_half(BLOCKS - 1, 1, e, w)
            second_half(BLOCKS - 2, 0, w_before)
            turn_hid(BLOCKS - 1, 1)
            second_half(BLOCKS - 1, 1, w)


_INS = {"x": "x", "src": "src", "dst": "dst", "typ": "edge_type_64", "query_emb": "L0_gnn_query_emb",
        "Wq": "L0_gnn_Wq", "bq": "L0_gnn_bq", "Wk": "L0_gnn_Wk", "bk": "L0_gnn_bk", "Wv": "L0_gnn_Wv", "bv": "L0_gnn_bv",
        "rel_w": "L0_gnn_rel_w", "Wo": "L0_gnn_Wo", "bo": "L0_gnn_bo", "gamma": "L0_gnn_gamma", "beta": "L0_gnn_beta",
        "gate_w": "L0_ffn_gate_w", "gate_b": "L0_ffn_gate_b", "w1": "L0_ffn_w1", "w2": "L0_ffn_w2", "w3": "L0_ffn_w3"}



def kernel(**inputs):
    import numpy as np
    import concourse.bacc as bacc
    from concourse.bass_utils import run_bass_kernel_spmd as run

    nc = bacc.Bacc("TRN2", target_bir_lowering=False, num_devices=1)
    pads = {"x": (XT * P, 0), "src": (ET * P, 0), "dst": (ET * P, NO_DST), "typ": (ET * P, 0)}
    arrays, A = {}, {}
    for name, given in _INS.items():
        a = np.ascontiguousarray(inputs[given])
        if name in pads:
            rows, fill = pads[name]
            padded = np.full((rows,) + a.shape[1:], fill, a.dtype)
            padded[:a.shape[0]] = a
            a = padded
        arrays[f"in_{name}"] = a
        A[name] = nc.dram_tensor(f"in_{name}", a.shape, mybir.dt.from_np(a.dtype), kind="ExternalInput").ap()
    out = nc.dram_tensor("out_0", (NP, D), F32, kind="ExternalOutput").ap()
    build(nc, A, out)
    r = run(nc, [arrays], core_ids=[0])
    return r.results[0]["out_0"][:N]
```
